# Optimizing a Trainium2 kernel written in Bass

```python
import numpy as np
import jax
import jax.numpy as jnp

def _softmax(x, axis=-1):
    return jax.nn.softmax(x, axis=axis)

def _gelu(x):
    return jax.nn.gelu(x, approximate=True)

def _silu(x):
    return jax.nn.silu(x)

def _sigmoid(x):
    return jax.nn.sigmoid(x)

def _layernorm(x, axis=-1, eps=1e-05):
    m = jnp.mean(x, axis=axis, keepdims=True)
    v = jnp.var(x, axis=axis, keepdims=True)
    return (x - m) / jnp.sqrt(v + eps)

def _scatter_add(tgt, idx, src, axis=0):
    return tgt.at[idx].add(src)

def _segment_sum(src, seg, n):
    return jax.ops.segment_sum(src, seg, n)
kernel_name = 'mk_dlrm_tower_d1_rec_r8_516cde'

def setup_inputs(seed: int=0):
    np.random.seed(seed)
    _w = jnp.asarray

    def _rec_inputs():
        import jax
        import jax.numpy as jnp
        _tk = jax.random.key(seed)
        dense_ctx = jax.random.normal(jax.random.fold_in(_tk, 190), (512, 16), jnp.float32)
        ids = jnp.stack([jax.random.randint(jax.random.fold_in(_tk, 200 + f), (512,), 0, v, jnp.int32) for f, v in enumerate([1000, 1000, 1250, 1000, 1000, 125000, 12500, 1000, 12500, 125000, 125000, 12500, 1000, 1000, 1250, 1250, 12500, 1000, 12500, 12500, 1250, 1000, 1000, 1000, 12500, 1250, 1000, 1250, 1000, 1000, 1000, 1000, 1000, 1000, 1250, 1250, 1000, 1000, 12500, 1000])], axis=1)
        tbl_0 = 0.05 * jax.random.normal(jax.random.fold_in(_tk, 500 + 0), (1000, 64), jnp.float32)
        tbl_1 = 0.05 * jax.random.normal(jax.random.fold_in(_tk, 500 + 1), (1000, 64), jnp.float32)
        tbl_2 = 0.05 * jax.random.normal(jax.random.fold_in(_tk, 500 + 2), (1250, 64), jnp.float32)
        tbl_3 = 0.05 * jax.random.normal(jax.random.fold_in(_tk, 500 + 3), (1000, 64), jnp.float32)
        tbl_4 = 0.05 * jax.random.normal(jax.random.fold_in(_tk, 500 + 4), (1000, 64), jnp.float32)
        tbl_5 = 0.05 * jax.random.normal(jax.random.fold_in(_tk, 500 + 5), (125000, 64), jnp.float32)
        tbl_6 = 0.05 * jax.random.normal(jax.random.fold_in(_tk, 500 + 6), (12500, 64), jnp.float32)
        tbl_7 = 0.05 * jax.random.normal(jax.random.fold_in(_tk, 500 + 7), (1000, 64), jnp.float32)
        tbl_8 = 0.05 * jax.random.normal(jax.random.fold_in(_tk, 500 + 8), (12500, 64), jnp.float32)
        tbl_9 = 0.05 * jax.random.normal(jax.random.fold_in(_tk, 500 + 9), (125000, 64), jnp.float32)
        tbl_10 = 0.05 * jax.random.normal(jax.random.fold_in(_tk, 500 + 10), (125000, 64), jnp.float32)
        tbl_11 = 0.05 * jax.random.normal(jax.random.fold_in(_tk, 500 + 11), (12500, 64), jnp.float32)
        tbl_12 = 0.05 * jax.random.normal(jax.random.fold_in(_tk, 500 + 12), (1000, 64), jnp.float32)
        tbl_13 = 0.05 * jax.random.normal(jax.random.fold_in(_tk, 500 + 13), (1000, 64), jnp.float32)
        tbl_14 = 0.05 * jax.random.normal(jax.random.fold_in(_tk, 500 + 14), (1250, 64), jnp.float32)
        tbl_15 = 0.05 * jax.random.normal(jax.random.fold_in(_tk, 500 + 15), (1250, 64), jnp.float32)
        tbl_16 = 0.05 * jax.random.normal(jax.random.fold_in(_tk, 500 + 16), (12500, 64), jnp.float32)
        tbl_17 = 0.05 * jax.random.normal(jax.random.fold_in(_tk, 500 + 17), (1000, 64), jnp.float32)
        tbl_18 = 0.05 * jax.random.normal(jax.random.fold_in(_tk, 500 + 18), (12500, 64), jnp.float32)
        tbl_19 = 0.05 * jax.random.normal(jax.random.fold_in(_tk, 500 + 19), (12500, 64), jnp.float32)
        tbl_20 = 0.05 * jax.random.normal(jax.random.fold_in(_tk, 500 + 20), (1250, 64), jnp.float32)
        tbl_21 = 0.05 * jax.random.normal(jax.random.fold_in(_tk, 500 + 21), (1000, 64), jnp.float32)
        tbl_22 = 0.05 * jax.random.normal(jax.random.fold_in(_tk, 500 + 22), (1000, 64), jnp.float32)
        tbl_23 = 0.05 * jax.random.normal(jax.random.fold_in(_tk, 500 + 23), (1000, 64), jnp.float32)
        tbl_24 = 0.05 * jax.random.normal(jax.random.fold_in(_tk, 500 + 24), (12500, 64), jnp.float32)
        tbl_25 = 0.05 * jax.random.normal(jax.random.fold_in(_tk, 500 + 25), (1250, 64), jnp.float32)
        tbl_26 = 0.05 * jax.random.normal(jax.random.fold_in(_tk, 500 + 26), (1000, 64), jnp.float32)
        tbl_27 = 0.05 * jax.random.normal(jax.random.fold_in(_tk, 500 + 27), (1250, 64), jnp.float32)
        tbl_28 = 0.05 * jax.random.normal(jax.random.fold_in(_tk, 500 + 28), (1000, 64), jnp.float32)
        tbl_29 = 0.05 * jax.random.normal(jax.random.fold_in(_tk, 500 + 29), (1000, 64), jnp.float32)
        tbl_30 = 0.05 * jax.random.normal(jax.random.fold_in(_tk, 500 + 30), (1000, 64), jnp.float32)
        tbl_31 = 0.05 * jax.random.normal(jax.random.fold_in(_tk, 500 + 31), (1000, 64), jnp.float32)
        tbl_32 = 0.05 * jax.random.normal(jax.random.fold_in(_tk, 500 + 32), (1000, 64), jnp.float32)
        tbl_33 = 0.05 * jax.random.normal(jax.random.fold_in(_tk, 500 + 33), (1000, 64), jnp.float32)
        tbl_34 = 0.05 * jax.random.normal(jax.random.fold_in(_tk, 500 + 34), (1250, 64), jnp.float32)
        tbl_35 = 0.05 * jax.random.normal(jax.random.fold_in(_tk, 500 + 35), (1250, 64), jnp.float32)
        tbl_36 = 0.05 * jax.random.normal(jax.random.fold_in(_tk, 500 + 36), (1000, 64), jnp.float32)
        tbl_37 = 0.05 * jax.random.normal(jax.random.fold_in(_tk, 500 + 37), (1000, 64), jnp.float32)
        tbl_38 = 0.05 * jax.random.normal(jax.random.fold_in(_tk, 500 + 38), (12500, 64), jnp.float32)
        tbl_39 = 0.05 * jax.random.normal(jax.random.fold_in(_tk, 500 + 39), (1000, 64), jnp.float32)
        _rk = jax.random.fold_in(_tk, 7)
        W_top1 = 0.0354441 * jax.random.normal(jax.random.fold_in(_tk, 801), (796, 512), jnp.float32)
        W_top2 = 0.0441942 * jax.random.normal(jax.random.fold_in(_tk, 802), (512, 256), jnp.float32)
        W_top3 = 0.0625 * jax.random.normal(jax.random.fold_in(_tk, 803), (256, 1), jnp.float32)
        b_top1 = jnp.zeros((512,), jnp.float32)
        b_top2 = jnp.zeros((256,), jnp.float32)
        return (dense_ctx, ids, tbl_0, tbl_1, tbl_2, tbl_3, tbl_4, tbl_5, tbl_6, tbl_7, tbl_8, tbl_9, tbl_10, tbl_11, tbl_12, tbl_13, tbl_14, tbl_15, tbl_16, tbl_17, tbl_18, tbl_19, tbl_20, tbl_21, tbl_22, tbl_23, tbl_24, tbl_25, tbl_26, tbl_27, tbl_28, tbl_29, tbl_30, tbl_31, tbl_32, tbl_33, tbl_34, tbl_35, tbl_36, tbl_37, tbl_38, tbl_39, W_top1, b_top1, W_top2, b_top2, W_top3)
    dense_ctx, ids, tbl_0, tbl_1, tbl_2, tbl_3, tbl_4, tbl_5, tbl_6, tbl_7, tbl_8, tbl_9, tbl_10, tbl_11, tbl_12, tbl_13, tbl_14, tbl_15, tbl_16, tbl_17, tbl_18, tbl_19, tbl_20, tbl_21, tbl_22, tbl_23, tbl_24, tbl_25, tbl_26, tbl_27, tbl_28, tbl_29, tbl_30, tbl_31, tbl_32, tbl_33, tbl_34, tbl_35, tbl_36, tbl_37, tbl_38, tbl_39, W_top1, b_top1, W_top2, b_top2, W_top3 = _rec_inputs()

    def _L0_rec_setup():
        import jax, jax.numpy as jnp
        import numpy as np

        def _pair_indices(num_fields):
            i_idx, j_idx = np.triu_indices(num_fields, k=1)
            return (jnp.asarray(i_idx), jnp.asarray(j_idx))
        key = jax.random.key(seed)
        k1, k2 = jax.random.split(key)
        B, F, D = (256, 40, 64)
        P = F * (F - 1) // 2
        x = jax.random.normal(k1, (B, F, D), dtype=jnp.float32)
        W = jax.random.normal(k2, (P, D, D), dtype=jnp.float32) * (1.0 / np.sqrt(D))
        return {'x': x, 'W': W}
    _L0_rec_all = _L0_rec_setup()
    _L0_rec_in = {k: v for k, v in _L0_rec_all.items() if k in ('W',)}
    del _L0_rec_all
    return {'dense_ctx': dense_ctx, 'ids': ids, 'tbl_0': tbl_0, 'tbl_1': tbl_1, 'tbl_2': tbl_2, 'tbl_3': tbl_3, 'tbl_4': tbl_4, 'tbl_5': tbl_5, 'tbl_6': tbl_6, 'tbl_7': tbl_7, 'tbl_8': tbl_8, 'tbl_9': tbl_9, 'tbl_10': tbl_10, 'tbl_11': tbl_11, 'tbl_12': tbl_12, 'tbl_13': tbl_13, 'tbl_14': tbl_14, 'tbl_15': tbl_15, 'tbl_16': tbl_16, 'tbl_17': tbl_17, 'tbl_18': tbl_18, 'tbl_19': tbl_19, 'tbl_20': tbl_20, 'tbl_21': tbl_21, 'tbl_22': tbl_22, 'tbl_23': tbl_23, 'tbl_24': tbl_24, 'tbl_25': tbl_25, 'tbl_26': tbl_26, 'tbl_27': tbl_27, 'tbl_28': tbl_28, 'tbl_29': tbl_29, 'tbl_30': tbl_30, 'tbl_31': tbl_31, 'tbl_32': tbl_32, 'tbl_33': tbl_33, 'tbl_34': tbl_34, 'tbl_35': tbl_35, 'tbl_36': tbl_36, 'tbl_37': tbl_37, 'tbl_38': tbl_38, 'tbl_39': tbl_39, 'W_top1': W_top1, 'b_top1': b_top1, 'W_top2': W_top2, 'b_top2': b_top2, 'W_top3': W_top3, 'L0_rec_W': _L0_rec_in['W']}

def reference(dense_ctx, ids, tbl_0, tbl_1, tbl_2, tbl_3, tbl_4, tbl_5, tbl_6, tbl_7, tbl_8, tbl_9, tbl_10, tbl_11, tbl_12, tbl_13, tbl_14, tbl_15, tbl_16, tbl_17, tbl_18, tbl_19, tbl_20, tbl_21, tbl_22, tbl_23, tbl_24, tbl_25, tbl_26, tbl_27, tbl_28, tbl_29, tbl_30, tbl_31, tbl_32, tbl_33, tbl_34, tbl_35, tbl_36, tbl_37, tbl_38, tbl_39, W_top1, b_top1, W_top2, b_top2, W_top3, L0_rec_W):
    import jax
    import jax.numpy as jnp

    def _L0_rec_ref(x, W):
        import jax, jax.numpy as jnp
        import numpy as np

        def _pair_indices(num_fields):
            i_idx, j_idx = np.triu_indices(num_fields, k=1)
            return (jnp.asarray(i_idx), jnp.asarray(j_idx))
        B, F, D = x.shape
        i_idx, j_idx = _pair_indices(F)
        vi = x[:, i_idx, :]
        vj = x[:, j_idx, :]
        viW = jnp.einsum('bpd,pde->bpe', vi, W)
        out = jnp.einsum('bpe,bpe->bp', viW, vj)
        return out
    e = jnp.stack([tbl_0[ids[:, 0]], tbl_1[ids[:, 1]], tbl_2[ids[:, 2]], tbl_3[ids[:, 3]], tbl_4[ids[:, 4]], tbl_5[ids[:, 5]], tbl_6[ids[:, 6]], tbl_7[ids[:, 7]], tbl_8[ids[:, 8]], tbl_9[ids[:, 9]], tbl_10[ids[:, 10]], tbl_11[ids[:, 11]], tbl_12[ids[:, 12]], tbl_13[ids[:, 13]], tbl_14[ids[:, 14]], tbl_15[ids[:, 15]], tbl_16[ids[:, 16]], tbl_17[ids[:, 17]], tbl_18[ids[:, 18]], tbl_19[ids[:, 19]], tbl_20[ids[:, 20]], tbl_21[ids[:, 21]], tbl_22[ids[:, 22]], tbl_23[ids[:, 23]], tbl_24[ids[:, 24]], tbl_25[ids[:, 25]], tbl_26[ids[:, 26]], tbl_27[ids[:, 27]], tbl_28[ids[:, 28]], tbl_29[ids[:, 29]], tbl_30[ids[:, 30]], tbl_31[ids[:, 31]], tbl_32[ids[:, 32]], tbl_33[ids[:, 33]], tbl_34[ids[:, 34]], tbl_35[ids[:, 35]], tbl_36[ids[:, 36]], tbl_37[ids[:, 37]], tbl_38[ids[:, 38]], tbl_39[ids[:, 39]]], axis=1)
    z = _L0_rec_ref(e, L0_rec_W)
    z = z.reshape(z.shape[0], -1)
    h = jnp.concatenate([z, dense_ctx], axis=1)
    h = jnp.maximum(h @ W_top1 + b_top1, 0.0)
    h = jnp.maximum(h @ W_top2 + b_top2, 0.0)
    y = h @ W_top3
    return y

_drawn_inputs = setup_inputs


def setup_inputs(seed=0):
    import zlib

    import numpy as np

    out = dict(_drawn_inputs(seed))
    spreads = {'b_top1': (0.0, 0.1), 'b_top2': (0.0, 0.1)}
    factors = {}
    for name, (base, spread) in spreads.items():
        noise = np.random.default_rng([zlib.crc32(name.encode()), seed]).standard_normal(out[name].shape)
        drawn = base * np.exp(spread * noise) if base else spread * noise
        out[name] = jnp.asarray(drawn.astype(out[name].dtype))
    for name, factor in factors.items():
        out[name] = (out[name] * factor).astype(out[name].dtype)
    return out
```

```python
from contextlib import ExitStack

import numpy as np

import concourse.bass as bass
from concourse import mybir

ALU = mybir.AluOpType
ACT = mybir.ActivationFunctionType
F32 = mybir.dt.float32
F32R = mybir.dt.float32r
I32 = mybir.dt.int32

P = 128
B = 512
BT = B // P
F = 40
D = 64
GF = 4
NG = F // GF
N_DENSE = 16
N1, N2 = 512, 256
M1, M2 = N1 // P, N2 // P

LEAVES = [(0, 1), (2, 3), (1, 2), (0, 2)]
INNER = [(1, 1), (0, 2), (3, 3)]

CHUNK = 8
W_SLOTS = 3
Y_SLOTS = 3
G_TILES = 8
BANK_QUADS = 16

POOL_SPLITS_FROM = 28


def plan_tiles():
    tiles, first, first_cd = [], [], []
    for g in range(NG):
        first.append(len(tiles))
        tiles += [(i, g, 0) for i in range(GF * g)]
        first_cd.append(len(tiles))
        tiles += [(i, g, 1) for i in range(GF * g)]
        tiles += [(GF * g + m, g, pair) for m, pair in INNER]
    return tiles, first, first_cd


TILES, FIRST_AB, FIRST_CD = plan_tiles()
NT = len(TILES)
STEPS = NT // 2
CHUNKS = -(-NT // CHUNK)
QUADS = -(-NT // 4)
BANKS = -(-QUADS // BANK_QUADS)
LAST_QUADS = QUADS - BANK_QUADS * (BANKS - 1)
DENSE_ROW = 2 * LAST_QUADS


def z_row(t, leaf):
    q = t // 4
    return q // BANK_QUADS, 32 * (t % 4) + 2 * (q % BANK_QUADS) + leaf


def plan_turns():
    turns = []
    turns_at = [[] for _ in range(STEPS)]
    splits_at = [[] for _ in range(STEPS)]
    for g in range(NG):
        a = GF * g
        halves = [[("leaves", g, 0), ("x", a), ("x", a + 1)],
                  [("x", a + 3), ("x", a + 2), ("leaves", g, 1), ("leaves", g, 2)]]
        for half, need in enumerate((FIRST_AB[g], FIRST_CD[g])):
            lead = 0 if g < 4 else 9
            at = need // 2 - lead
            splits_at[max(at - 2, 0) if lead else at].append((g, half))
            for n, turn in enumerate(halves[half]):
                turns_at[at + (n if lead else 0)].append(len(turns))
                turns.append(turn)
    return turns, turns_at, splits_at


TURNS, TURNS_AT, SPLITS_AT = plan_turns()
TURN_OF = {turn: n for n, turn in enumerate(TURNS)}
ORDERED = [n for at in TURNS_AT for n in at]
TURN_SEQ = {n: k for k, n in enumerate(ORDERED)}
SPLITS = [s for at in SPLITS_AT for s in at]
SPLIT_SEQ = {s: k for k, s in enumerate(SPLITS)}


def turns_until(turn):
    if turn[0] == "leaves" and turn[2] == 3:
        turn = ("leaves", turn[1], 2)
    return TURN_SEQ[TURN_OF[turn]] + 1


def group_turns_until(g):
    return 1 + max(TURN_SEQ[n] for n, t in enumerate(TURNS)
                   if (t[1] // GF if t[0] == "x" else t[1]) == g)


LAST_STEP_OF_GROUP = [(FIRST_AB[g + 1] - 1) // 2 if g + 1 < NG else STEPS - 1 for g in range(NG)]


def dlrm_tower(nc, ids, tables, dense_t, w_pairs, w1, b1, w2, b2, w3, out):
    ctx = ExitStack()
    with ctx:
        def sb(name, shape, dt=F32):
            return ctx.enter_context(nc.sbuf_tensor(name, shape, dt))

        def ps(name, shape):
            return ctx.enter_context(nc.psum_tensor(name, shape, F32))

        def sem(name):
            return ctx.enter_context(nc.semaphore(name))

        ids_sb = sb("ids_sb", [P, BT, F], I32)
        ident = sb("ident", [P, P])
        selector = sb("selector", [P, 62])
        rows = sb("rows", [P, 2, BT, GF * D])
        parts = sb("parts", [P, 2, BT, GF, 2 * D])
        x_mov = sb("x_mov", [P, F, B], F32R)
        x_leaf = sb("x_leaf", [P, 2, len(LEAVES), B])
        w_raw = sb("w_raw", [P, W_SLOTS, CHUNK * P])
        w_high = sb("w_high", [P, W_SLOTS, CHUNK * P], F32R)
        w_low = sb("w_low", [P, W_SLOTS, CHUNK * P], F32R)
        prod = sb("prod", [P, G_TILES, B])
        z_sb = sb("z_sb", [P, BANKS, B])
        w1_sb = sb("w1_sb", [P, BANKS, N1])
        w2_sb = sb("w2_sb", [P, M1, N2])
        w3_sb = sb("w3_sb", [P, M2])
        b1_sb = sb("b1_sb", [P, M1])
        b2_sb = sb("b2_sb", [P, M2])
        h1_sb = prod[:, 0:M1, :]
        h2_sb = prod[:, M1:M1 + M2, :]
        y_sb = prod[0:1, M1 + M2, :]

        y_ps = ps("y_ps", [P, Y_SLOTS, 2, B])
        z_ps = ps("z_ps", [P, B])
        t_ps = ps("t_ps", [P, B])
        h1_ps = [y_ps[:, m // 2, m % 2, :] for m in range(M1)]
        h2_ps = [y_ps[:, 2, m, :] for m in range(M2)]
        out_ps = t_ps[0:1, :]

        ids_loaded = sem("ids_loaded")
        gathered = [[sem(f"gathered{s}_{h}") for h in range(2)] for s in range(2)]
        w_loaded = [sem(f"w_loaded{s}") for s in range(W_SLOTS)]
        mlp_loaded = sem("mlp_loaded")
        dense_loaded = sem("dense_loaded")
        ident_zeroed = sem("ident_zeroed")
        ident_ready = sem("ident_ready")
        selector_zeroed = sem("selector_zeroed")
        selector_ready = sem("selector_ready")
        z_zeroed = sem("z_zeroed")
        rows_high = sem("rows_high")
        rows_low = sem("rows_low")
        w_high_made = sem("w_high_made")
        w_low_made = sem("w_low_made")
        w_low_pool = sem("w_low_pool")
        turned = sem("turned")
        turn_copied = sem("turn_copied")
        y_ready = sem("y_ready")
        prod_ready = sem("prod_ready")
        quad_summed = sem("quad_summed")
        z_saved = sem("z_saved")
        h1_summed = sem("h1_summed")
        h1_ready = sem("h1_ready")
        h2_summed = sem("h2_summed")
        h2_ready = sem("h2_ready")
        out_summed = sem("out_summed")
        out_ready = sem("out_ready")
        out_stored = sem("out_stored")

        def wait_low(eng, c):
            if c < POOL_SPLITS_FROM:
                eng.wait_ge(w_low_made, c + 1)
            else:
                eng.wait_ge(w_low_pool, c + 1 - POOL_SPLITS_FROM)

        def make_low(eng, c):
            s = c % W_SLOTS
            eng.wait_ge(w_high_made, c + 1)
            if c >= W_SLOTS:
                eng.wait_ge(y_ready, CHUNK // 2 * (c - W_SLOTS + 1))
            return eng.tensor_tensor(w_low[:, s, :], w_raw[:, s, :], w_high[:, s, :].bitcast(F32),
                                     ALU.subtract)

        block = ctx.enter_context(nc.Block())

        @block.sync
        def _(sp):
            sp.dma_start(ids_sb[:], ids.rearrange("(t p) f -> p t f", p=P)).then_inc(ids_loaded, 16)
            for c in range(CHUNKS):
                if c >= W_SLOTS:
                    sp.wait_ge(w_high_made, c - W_SLOTS + 1)
                    wait_low(sp, c - W_SLOTS)
                for half in range(2):
                    sp.dma_start(w_raw[D * half:D * half + D, c % W_SLOTS, :],
                                 w_pairs[c]).then_inc(w_loaded[c % W_SLOTS], 16)
                if c == 6:
                    sp.wait_ge(z_zeroed, 1)
                    sp.dma_start(z_sb[DENSE_ROW:DENSE_ROW + N_DENSE, BANKS - 1, :],
                                 dense_t).then_inc(dense_loaded, 16)
                if c == 12:
                    sp.dma_start(w1_sb[:], w1).then_inc(mlp_loaded, 16)
                    sp.dma_start(w2_sb[:], w2).then_inc(mlp_loaded, 16)
                    sp.dma_start(w3_sb[:], w3).then_inc(mlp_loaded, 16)
                    sp.dma_start(b1_sb[:], b1).then_inc(mlp_loaded, 16)
                    sp.dma_start(b2_sb[:], b2).then_inc(mlp_loaded, 16)
            sp.wait_ge(out_ready, 1)
            sp.dma_start(out.rearrange("b o -> o b"), y_sb).then_inc(out_stored, 16)
            sp.wait_ge(out_stored, 16)

        @block.gpsimd
        def _(pool):
            pool.memset(ident[:], 0.0).then_inc(ident_zeroed, 1)
            pool.wait_ge(ident_zeroed, 1)
            pool.affine_select(out=ident[:], in_=ident[:], compare_op=ALU.not_equal, fill=1.0, base=0,
                               pattern=[[-1, P]], channel_multiplier=1).then_inc(ident_ready, 1)
            pool.wait_ge(ids_loaded, 16)
            for g in range(NG):
                if g >= 2:
                    pool.wait_ge(turned, group_turns_until(g - 2))
                for f in range(GF):
                    for bt in range(BT):
                        pool.indirect_dma_start(
                            rows[:, g % 2, bt, f * D:(f + 1) * D], None, tables[GF * g + f],
                            bass.IndirectOffsetOnAxis(
                                ap=ids_sb[:, bt, GF * g + f:GF * g + f + 1], axis=0),
                        ).then_inc(gathered[g % 2][f // 2], 16)
            for c in range(POOL_SPLITS_FROM, CHUNKS):
                make_low(pool, c).then_inc(w_low_pool, 1)

        @block.scalar
        def _(act):
            def high_weights(c):
                s = c % W_SLOTS
                act.wait_ge(w_loaded[s], 32 * (c // W_SLOTS + 1))
                if c >= W_SLOTS:
                    act.wait_ge(y_ready, CHUNK // 2 * (c - W_SLOTS + 1))
                act.activation(w_high[:, s, :], w_raw[:, s, :], ACT.Copy).then_inc(w_high_made, 1)

            def high_rows(g, half):
                act.wait_ge(gathered[g % 2][half], 16 * 2 * BT * (g // 2 + 1))
                if g >= 2:
                    act.wait_ge(turned, group_turns_until(g - 2))
                act.activation(parts[:, g % 2, :, 2 * half:2 * half + 2, 0:D].bitcast(F32R),
                               rows[:, g % 2, :, 2 * D * half:2 * D * half + 2 * D]
                               .rearrange("p t (f d) -> p t f d", d=D), ACT.Copy).then_inc(rows_high, 1)

            def copy_turn(n):
                turn = TURNS[n]
                act.wait_ge(turned, TURN_SEQ[n] + 1)
                if turn[0] == "x":
                    dst = x_mov[:, turn[1], :]
                else:
                    g = turn[1]
                    if g >= 2:
                        act.wait_ge(prod_ready, LAST_STEP_OF_GROUP[g - 2] + 1)
                    dst = x_leaf[:, g % 2, turn[2], :]
                    if turn[2] in (0, 2):
                        h = D * (turn[2] // 2)
                        act.activation(x_leaf[h:h + D, g % 2, 3, :], t_ps[h:h + D, :], ACT.Copy)
                act.activation(dst, t_ps[:], ACT.Copy).then_inc(turn_copied, 1)

            high_weights(0)
            high_weights(1)
            for s in range(STEPS):
                if s % (CHUNK // 2) == 0 and s // (CHUNK // 2) + 2 < CHUNKS:
                    high_weights(s // (CHUNK // 2) + 2)
                for g, half in SPLITS_AT[s]:
                    high_rows(g, half)
                for n in TURNS_AT[s]:
                    copy_turn(n)
                quad = s // 2 - 1
                if s % 2 and quad >= 0 and quad % BANK_QUADS == BANK_QUADS - 1:
                    act.wait_ge(quad_summed, quad + 1)
                    act.activation(z_sb[:, quad // BANK_QUADS, :], z_ps[:], ACT.Copy).then_inc(z_saved, 1)
            act.wait_ge(quad_summed, QUADS)
            act.wait_ge(dense_loaded, 16)
            for c in range(4):
                act.activation(z_sb[32 * c:32 * c + 2 * LAST_QUADS, BANKS - 1, :],
                               z_ps[32 * c:32 * c + 2 * LAST_QUADS, :], ACT.Copy).then_inc(z_saved, 1)
            act.wait_ge(mlp_loaded, 80)
            for m in range(M1):
                act.wait_ge(h1_summed, m + 1)
                act.activation(h1_sb[:, m, :], h1_ps[m], ACT.Relu, bias=b1_sb[:, m:m + 1]).then_inc(h1_ready, 1)
            for m in range(M2):
                act.wait_ge(h2_summed, m + 1)
                act.activation(h2_sb[:, m, :], h2_ps[m], ACT.Relu, bias=b2_sb[:, m:m + 1]).then_inc(h2_ready, 1)
            act.wait_ge(out_summed, 1)
            act.activation(y_sb, out_ps, ACT.Copy).then_inc(out_ready, 1)

        @block.vector
        def _(dve):
            dve.memset(selector[:], 0.0).then_inc(selector_zeroed, 1)
            dve.memset(z_sb[:, BANKS - 1, :], 0.0).then_inc(z_zeroed, 1)
            dve.wait_ge(selector_zeroed, 1)
            dve.memset(selector[0:D, 30:31], 1.0).then_inc(selector_ready, 1)
            dve.memset(selector[D:P, 31:32], 1.0).then_inc(selector_ready, 1)

            def low_rows(g, half):
                dve.wait_ge(rows_high, SPLIT_SEQ[(g, half)] + 1)
                dve.tensor_tensor(parts[:, g % 2, :, 2 * half:2 * half + 2, D:2 * D],
                                  rows[:, g % 2, :, 2 * D * half:2 * D * half + 2 * D]
                                  .rearrange("p t (f d) -> p t f d", d=D),
                                  parts[:, g % 2, :, 2 * half:2 * half + 2, 0:D],
                                  ALU.subtract).then_inc(rows_low, 1)

            def multiply(s):
                q = s // 2
                dve.wait_ge(y_ready, s + 1)
                if q >= 2:
                    dve.wait_ge(quad_summed, q - 1)
                pair = [TILES[2 * s], TILES[2 * s + 1]]
                for _, g, leaves in pair:
                    dve.wait_ge(turn_copied, turns_until(("leaves", g, leaves)))
                at = (2 * s) % G_TILES
                if pair[0][1:] == pair[1][1:]:
                    _, g, leaves = pair[0]
                    both = x_leaf[:, g % 2, leaves:leaves + 1, :].to_broadcast([P, 2, B])
                    ins = dve.tensor_tensor(prod[:, at:at + 2, :], y_ps[:, s % Y_SLOTS], both, ALU.mult)
                else:
                    for n, (_, g, leaves) in enumerate(pair):
                        ins = dve.tensor_tensor(prod[:, at + n, :], y_ps[:, s % Y_SLOTS, n, :],
                                                x_leaf[:, g % 2, leaves, :], ALU.mult)
                ins.then_inc(prod_ready, 1)

            for c in range(2):
                make_low(dve, c).then_inc(w_low_made, 1)
            for s in range(STEPS):
                c = s // (CHUNK // 2) + 2
                if s % (CHUNK // 2) == 0 and c < POOL_SPLITS_FROM:
                    make_low(dve, c).then_inc(w_low_made, 1)
                for g, half in SPLITS_AT[s]:
                    low_rows(g, half)
                multiply(s)

        @block.tensor
        def _(pe):
            def turn(n):
                what = TURNS[n]
                k = TURN_SEQ[n]
                if k:
                    pe.wait_ge(turn_copied, k)
                if what[0] == "x":
                    g, f = divmod(what[1], GF)
                    pe.wait_ge(rows_low, SPLIT_SEQ[(g, f // 2)] + 1)
                    src = [parts[:, g % 2, bt, f, :] for bt in range(BT)]
                else:
                    g = what[1]
                    f0, f1 = LEAVES[what[2]]
                    pe.wait_ge(rows_high, SPLIT_SEQ[(g, f1 // 2)] + 1)
                    src = [rows[:, g % 2, bt, f0 * D:(f1 + 1) * D] for bt in range(BT)]
                for bt in range(BT):
                    ins = pe.transpose(t_ps[:, P * bt:P * bt + P], src[bt], ident[:])
                ins.then_inc(turned, 1)

            def tiles(s):
                c = 2 * s // CHUNK
                if s % (CHUNK // 2) == 0:
                    pe.wait_ge(w_high_made, c + 1)
                    wait_low(pe, c)
                if s >= Y_SLOTS:
                    pe.wait_ge(prod_ready, s - Y_SLOTS + 1)
                for n in range(2):
                    mover = TILES[2 * s + n][0]
                    pe.wait_ge(turn_copied, turns_until(("x", mover)))
                    at = P * ((2 * s + n) % CHUNK)
                    for k, w in enumerate((w_high, w_low)):
                        ins = pe.matmul(y_ps[:, s % Y_SLOTS, n, :], w[:, c % W_SLOTS, at:at + P],
                                        x_mov[:, mover, :], start=(k == 0), stop=(k == 1))
                ins.then_inc(y_ready, 1)

            def sum_quad(q):
                r = q % BANK_QUADS
                n = min(4, NT - 4 * q)
                pe.wait_ge(prod_ready, 2 * q + (n + 1) // 2)
                if q == 0:
                    pe.wait_ge(selector_ready, 2)
                elif r == 0:
                    pe.wait_ge(z_saved, q // BANK_QUADS)
                for c in range(n):
                    last = r == BANK_QUADS - 1 or 4 * (q + 1) + c >= NT
                    ins = pe.matmul(z_ps[32 * c:32 * c + 32, :], selector[:, 30 - 2 * r:62 - 2 * r],
                                    prod[:, (4 * q + c) % G_TILES, :], start=(r == 0), stop=last)
                ins.then_inc(quad_summed, 1)

            pe.wait_ge(ident_ready, 1)
            for s in range(STEPS):
                for n in TURNS_AT[s]:
                    turn(n)
                tiles(s)
                if s % 2 and s >= 3:
                    sum_quad(s // 2 - 1)
            for q in range((STEPS - 1) // 2 - 1 + (STEPS % 2 == 0), QUADS):
                sum_quad(q)

            pe.wait_ge(mlp_loaded, 80)
            pe.wait_ge(prod_ready, STEPS)
            for b in range(BANKS):
                pe.wait_ge(z_saved, b + 1 if b < BANKS - 1 else b + 4)
                for m in range(M1):
                    ins = pe.matmul(h1_ps[m], w1_sb[:, b, P * m:P * m + P], z_sb[:, b, :],
                                    start=(b == 0), stop=(b == BANKS - 1))
                    if b == BANKS - 1:
                        ins.then_inc(h1_summed, 1)
            for k in range(M1):
                pe.wait_ge(h1_ready, k + 1)
                for m in range(M2):
                    ins = pe.matmul(h2_ps[m], w2_sb[:, k, P * m:P * m + P], h1_sb[:, k, :],
                                    start=(k == 0), stop=(k == M1 - 1))
                    if k == M1 - 1:
                        ins.then_inc(h2_summed, 1)
            for k in range(M2):
                pe.wait_ge(h2_ready, k + 1)
                ins = pe.matmul(out_ps, w3_sb[:, k:k + 1], h2_sb[:, k, :], start=(k == 0), stop=(k == M2 - 1))
            ins.then_inc(out_summed, 1)


def lay_out_pairs(w):
    number = {p: n for n, p in enumerate(zip(*np.triu_indices(F, k=1)))}
    laid = np.zeros((CHUNKS, D, CHUNK, 2, D), w.dtype)
    for t, (i, g, pair) in enumerate(TILES):
        for leaf, f in enumerate(LEAVES[pair]):
            j = GF * g + f
            m = w[number[(i, j)]] if i < j else w[number[(j, i)]].T
            laid[t // CHUNK, :, t % CHUNK, leaf, :] = m
    return laid.reshape(CHUNKS, D, CHUNK * P)


def lay_out_top1(w):
    number = {p: n for n, p in enumerate(zip(*np.triu_indices(F, k=1)))}
    laid = np.zeros((P, BANKS, N1), w.dtype)
    for t, (i, g, pair) in enumerate(TILES):
        for leaf, f in enumerate(LEAVES[pair]):
            j = GF * g + f
            bank, row = z_row(t, leaf)
            laid[row, bank] = w[number[(min(i, j), max(i, j))]]
    laid[DENSE_ROW:DENSE_ROW + N_DENSE, BANKS - 1] = w[len(number):]
    return laid


def kernel(**inputs):
    import concourse.bacc as _bacc
    from concourse.bass_utils import run_bass_kernel_spmd as _run

    a = {name: np.ascontiguousarray(x) for name, x in inputs.items()}
    arrays = {
        "in_ids": a["ids"],
        **{f"in_tbl_{f}": a[f"tbl_{f}"] for f in range(F)},
        "in_dense_t": np.ascontiguousarray(a["dense_ctx"].T),
        "in_w_pairs": lay_out_pairs(a["L0_rec_W"]),
        "in_w1": lay_out_top1(a["W_top1"]),
        "in_b1": np.ascontiguousarray(a["b_top1"].reshape(M1, P).T),
        "in_w2": np.ascontiguousarray(a["W_top2"].reshape(M1, P, N2).transpose(1, 0, 2)),
        "in_b2": np.ascontiguousarray(a["b_top2"].reshape(M2, P).T),
        "in_w3": np.ascontiguousarray(a["W_top3"].reshape(M2, P).T),
    }
    nc = _bacc.Bacc("TRN2", target_bir_lowering=False, num_devices=1)
    ap = {name: nc.dram_tensor(name, x.shape, mybir.dt.from_np(x.dtype), kind="ExternalInput").ap()
          for name, x in arrays.items()}
    out = nc.dram_tensor("out_y", (B, 1), F32, kind="ExternalOutput").ap()
    dlrm_tower(nc, ap["in_ids"], [ap[f"in_tbl_{f}"] for f in range(F)], ap["in_dense_t"], ap["in_w_pairs"],
               ap["in_w1"], ap["in_b1"], ap["in_w2"], ap["in_b2"], ap["in_w3"], out)
    r = _run(nc, [arrays], core_ids=[0])
    return r.results[0]["out_y"]
```

```python
from contextlib import ExitStack

import numpy as np

import concourse.bass as bass
from concourse import mybir

ALU = mybir.AluOpType
ACT = mybir.ActivationFunctionType
F32 = mybir.dt.float32
F32R = mybir.dt.float32r
I32 = mybir.dt.int32

P = 128
B = 512
BT = B // P
F = 40
D = 64
GF = 4
NG = F // GF
N_DENSE = 16
N1, N2 = 512, 256
M1, M2 = N1 // P, N2 // P

AB, CD, BC, AC, EVEN, ODD = range(6)
FIELDS_OF = {AB: (0, 1), CD: (2, 3), BC: (1, 2), AC: (0, 2)}
LEAF_AT = {AB: 0, EVEN: 0, ODD: 1, CD: 2, BC: 3, AC: 4}
N_LEAF = 5

CHUNK = 8
RAW_SLOTS = 2
W_SLOTS = 3
Y_SLOTS = 3
G_UNITS = 8
ROW_SLOTS = 4
ROUND = 4
BANK_ROUNDS = 8
SUM_LAG = 3

HALVED_GROUPS = 4
INNER_AFTER = 10
LEAF_LEAD = 3
POOL_SPLITS_FROM = 21
ADDED_ROUNDS = list(range(17,49,2))
POOL_TURNS = (0,2)


def plan_units():
    units, first, first_cd = [], [], []
    for g in range(NG):
        a, movers = GF * g, range(GF * g)
        first.append(len(units))
        inner = [((a - 1, g - 1, AC), (a + 3, g, AC))] if g % 2 else []
        inner.append(((a + 1, g, CD), (a, g, BC)))
        if g < HALVED_GROUPS:
            units += [((i, g, AB), (i + 1, g, AB)) for i in movers[::2]]
            first_cd.append(len(units))
            cross = [((i, g, CD), (i + 1, g, CD)) for i in movers[::2]]
            after = len(cross) if g + 1 < HALVED_GROUPS else len(cross) - LEAF_LEAD
        else:
            first_cd.append(len(units))
            cross = [((i, g, EVEN), (i, g, ODD)) for i in movers]
            after = INNER_AFTER
        units += cross[:after] + inner + cross[after:]
    return units, first, first_cd


UNITS, FIRST_AB, FIRST_CD = plan_units()
STEPS = len(UNITS)
TILES = [tile for unit in UNITS for tile in unit]
NT = len(TILES)
CHUNKS = -(-NT // CHUNK)
ROUNDS = -(-STEPS // ROUND)
BANKS = -(-ROUNDS // BANK_ROUNDS)
LAST_UNITS = STEPS - ROUND * BANK_ROUNDS * (BANKS - 1)
assert LAST_UNITS <= ROUND
DENSE_ROW = 4


ADDS = [u for u in range(STEPS) if u // ROUND in ADDED_ROUNDS and UNITS[u][0][2] == EVEN]
POOL_ADDS = [u for u in ADDS if u % ROUND in POOL_TURNS]
DVE_ADDS = [u for u in ADDS if u % ROUND not in POOL_TURNS]


def pairs_of(t):
    mover, g, kind = TILES[t]
    if kind in FIELDS_OF:
        return [(mover, GF * g + f, slice(D * n, D * n + D), slice(0, D), 2 * (t % 2) + n)
                for n, f in enumerate(FIELDS_OF[kind])]
    return [(mover, GF * g + f, slice(D // 2 * f, D // 2 * (f + 1)), slice(kind - EVEN, D, 2), f)
            for f in range(GF)]


def z_row(u, n):
    r = u // ROUND
    return r // BANK_ROUNDS, 32 * (u % ROUND) + 4 * (r % BANK_ROUNDS) + n


def plan_jobs():
    jobs_at = [[] for _ in range(STEPS)]
    for g in range(NG):
        a, f, cd = GF * g, FIRST_AB[g], FIRST_CD[g]
        if g < HALVED_GROUPS:
            jobs = [(f, ("leaves", g, AB)), (f, ("split", g, 0)), (f + 1, ("x", a)), (f + 2, ("x", a + 1)),
                    (cd, ("leaves", g, CD)), (cd, ("split", g, 1)), (cd + 1, ("x", a + 3)),
                    (cd + 2, ("leaves", g, BC)), (cd + 3, ("x", a + 2))]
        else:
            turns = [("leaves", g, EVEN), ("leaves", g, ODD), ("leaves", g, AB), ("leaves", g, BC),
                     ("leaves", g, CD), ("x", a + 3), ("x", a), ("x", a + 1), ("x", a + 2)]
            jobs = [(f - LEAF_LEAD + n, turn) for n, turn in enumerate(turns)]
            jobs[3:3] = [(f, ("split", g, 0)), (f, ("split", g, 1))]
        for at, job in jobs:
            jobs_at[min(at, needed(job))].append(job)
    return jobs_at


def needed(job):
    if job[0] == "split":
        return STEPS
    uses = [s for s, unit in enumerate(UNITS) for i, g, kind in unit
            if job == ("x", i) or job == ("leaves", g, kind)
            or (job[0] == "leaves" and job[1] == g and kind == AC and job[2] in (AB, BC))]
    return min(uses, default=STEPS)


JOBS_AT = plan_jobs()
JOBS = [job for at in JOBS_AT for job in at]
TURN_SEQ = {turn: n for n, turn in enumerate(j for j in JOBS if j[0] != "split")}
SPLIT_SEQ = {split[1:]: n for n, split in enumerate(j for j in JOBS if j[0] == "split")}


def turns_until(turn):
    if turn[0] == "leaves" and turn[2] == AC:
        turn = ("leaves", turn[1], BC)
    return TURN_SEQ[turn] + 1


def group_turns_until(g):
    return 1 + max(n for t, n in TURN_SEQ.items() if (t[1] // GF if t[0] == "x" else t[1]) == g)


LAST_STEP_OF_LEAVES = [max(s for s, unit in enumerate(UNITS) if any(t[1] == g for t in unit))
                       for g in range(NG)]
for _s, _jobs in enumerate(JOBS_AT):
    for _t in _jobs:
        assert _t[0] != "leaves" or _t[1] < 2 or LAST_STEP_OF_LEAVES[_t[1] - 2] < _s, (_t, _s)


def dlrm_tower(nc, ids, tables, dense_t, w_pairs, w1, b1, w2, b2, w3, out):
    ctx = ExitStack()
    with ctx:
        def sb(name, shape, dt=F32):
            return ctx.enter_context(nc.sbuf_tensor(name, shape, dt))

        def ps(name, shape):
            return ctx.enter_context(nc.psum_tensor(name, shape, F32))

        def sem(name):
            return ctx.enter_context(nc.semaphore(name))

        ids_sb = sb("ids_sb", [P, BT, F], I32)
        ident = sb("ident", [P, P])
        selector2 = sb("selector2", [P, 62])
        selector4 = sb("selector4", [P, 60])
        rows = sb("rows", [P, ROW_SLOTS, BT, GF * D])
        parts = sb("parts", [P, 2, BT, 2, 2 * D])
        x_mov = sb("x_mov", [P, F, B], F32R)
        x_leaf = sb("x_leaf", [P, 2, N_LEAF, B])
        w_raw = sb("w_raw", [P, RAW_SLOTS, CHUNK * P])
        w_high = sb("w_high", [P, W_SLOTS, CHUNK * P], F32R)
        w_low = sb("w_low", [P, W_SLOTS, CHUNK * P], F32R)
        prod = sb("prod", [P, 2 * G_UNITS, B])
        z_sb = sb("z_sb", [P, BANKS, B])
        w2_sb = sb("w2_sb", [P, M1, N2])
        w3_sb = sb("w3_sb", [P, M2])
        b1_sb = sb("b1_sb", [P, M1])
        b2_sb = sb("b2_sb", [P, M2])
        w1_sb = rows[:].rearrange("p s t n -> p (s t n)")[:, 0:BANKS * N1].rearrange("p (b n) -> p b n", n=N1)
        h1_sb = prod[:, 0:M1, :]
        h2_sb = prod[:, M1:M1 + M2, :]
        y_sb = prod[0:1, M1 + M2, :]

        y_ps = ps("y_ps", [P, Y_SLOTS, 2, B])
        z_ps = ps("z_ps", [P, B])
        t_ps = ps("t_ps", [P, B])
        h1_ps = [y_ps[:, m // 2, m % 2, :] for m in range(M1)]
        h2_ps = [y_ps[:, 2, m, :] for m in range(M2)]
        out_ps = t_ps[0:1, :]

        ids_loaded = sem("ids_loaded")
        gathered = [[sem(f"gathered{s}_{h}") for h in range(2)] for s in range(ROW_SLOTS)]
        w_loaded = [sem(f"w_loaded{s}") for s in range(RAW_SLOTS)]
        w1_loaded = sem("w1_loaded")
        mlp_loaded = sem("mlp_loaded")
        dense_loaded = sem("dense_loaded")
        ident_zeroed = sem("ident_zeroed")
        ident_ready = sem("ident_ready")
        selector_zeroed = sem("selector_zeroed")
        selector_ready = sem("selector_ready")
        z_zeroed = sem("z_zeroed")
        rows_high = sem("rows_high")
        rows_low = sem("rows_low")
        w_high_made = sem("w_high_made")
        w_low_made = sem("w_low_made")
        w_low_pool = sem("w_low_pool")
        turned = sem("turned")
        turn_copied = sem("turn_copied")
        y_ready = sem("y_ready")
        prod_ready = sem("prod_ready")
        added_dve = sem("added_dve")
        added_pool = sem("added_pool")
        round_summed = sem("round_summed")
        z_saved = sem("z_saved")
        h1_summed = sem("h1_summed")
        h1_ready = sem("h1_ready")
        h2_summed = sem("h2_summed")
        h2_ready = sem("h2_ready")
        out_summed = sem("out_summed")
        out_ready = sem("out_ready")
        out_stored = sem("out_stored")

        def wait_low(eng, c):
            if c < POOL_SPLITS_FROM:
                eng.wait_ge(w_low_made, c + 1)
            else:
                eng.wait_ge(w_low_pool, c + 1 - POOL_SPLITS_FROM)

        def make_low(eng, c):
            s = c % W_SLOTS
            eng.wait_ge(w_high_made, c + 1)
            if c >= W_SLOTS:
                eng.wait_ge(y_ready, CHUNK // 2 * (c - W_SLOTS + 1))
            return eng.tensor_tensor(w_low[:, s, :], w_raw[:, c % RAW_SLOTS, :], w_high[:, s, :].bitcast(F32),
                                     ALU.subtract)

        def wait_gathered(eng, g, half):
            eng.wait_ge(gathered[g % ROW_SLOTS][half], 16 * 2 * BT * (g // ROW_SLOTS + 1))

        def rows_of(g, half):
            return rows[:, g % ROW_SLOTS, :, 2 * D * half:2 * D * half + 2 * D].rearrange(
                "p t (f d) -> p t f d", d=D)

        def wait_parts_free(eng, k):
            if k >= 2:
                g, half = [split for split, n in SPLIT_SEQ.items() if n == k - 2][0]
                eng.wait_ge(turned, max(turns_until(("x", GF * g + 2 * half + f)) for f in range(2)))

        def round_at(s):
            r, rest = divmod(s - SUM_LAG - (ROUND - 1), ROUND)
            return r if rest == 0 and r >= 0 else None

        def add_halves(eng, u):
            at = 2 * (u % G_UNITS)
            eng.wait_ge(prod_ready, u + 1)
            return eng.tensor_tensor(prod[:, at, :], prod[:, at, :], prod[:, at + 1, :], ALU.add)

        block = ctx.enter_context(nc.Block())

        @block.sync
        def _(sp):
            sp.dma_start(ids_sb[:], ids.rearrange("(t p) f -> p t f", p=P)).then_inc(ids_loaded, 16)
            for c in range(CHUNKS):
                if c >= RAW_SLOTS:
                    wait_low(sp, c - RAW_SLOTS)
                for half in range(2):
                    sp.dma_start(w_raw[D * half:D * half + D, c % RAW_SLOTS, :],
                                 w_pairs[c]).then_inc(w_loaded[c % RAW_SLOTS], 16)
                if c == 6:
                    sp.wait_ge(z_zeroed, 1)
                    sp.dma_start(z_sb[DENSE_ROW:DENSE_ROW + N_DENSE, BANKS - 1, :],
                                 dense_t).then_inc(dense_loaded, 16)
                if c == 12:
                    sp.dma_start(w2_sb[:], w2).then_inc(mlp_loaded, 16)
                    sp.dma_start(w3_sb[:], w3).then_inc(mlp_loaded, 16)
                    sp.dma_start(b1_sb[:], b1).then_inc(mlp_loaded, 16)
                    sp.dma_start(b2_sb[:], b2).then_inc(mlp_loaded, 16)
            sp.wait_ge(turned, len(TURN_SEQ))
            sp.dma_start(w1_sb, w1).then_inc(w1_loaded, 16)
            sp.wait_ge(out_ready, 1)
            sp.dma_start(out.rearrange("b o -> o b"), y_sb).then_inc(out_stored, 16)
            sp.wait_ge(out_stored, 16)

        @block.gpsimd
        def _(pool):
            pool.memset(ident[:], 0.0).then_inc(ident_zeroed, 1)
            pool.wait_ge(ident_zeroed, 1)
            pool.affine_select(out=ident[:], in_=ident[:], compare_op=ALU.not_equal, fill=1.0, base=0,
                               pattern=[[-1, P]], channel_multiplier=1).then_inc(ident_ready, 1)
            pool.wait_ge(ids_loaded, 16)
            for g in range(NG):
                if g >= ROW_SLOTS:
                    pool.wait_ge(turned, group_turns_until(g - ROW_SLOTS))
                for f in range(GF):
                    for bt in range(BT):
                        pool.indirect_dma_start(
                            rows[:, g % ROW_SLOTS, bt, f * D:(f + 1) * D], None, tables[GF * g + f],
                            bass.IndirectOffsetOnAxis(
                                ap=ids_sb[:, bt, GF * g + f:GF * g + f + 1], axis=0),
                        ).then_inc(gathered[g % ROW_SLOTS][f // 2], 16)
            for s in range(STEPS):
                c, rest = divmod(s, CHUNK // 2)
                if rest == 0 and POOL_SPLITS_FROM <= c + 2 < CHUNKS:
                    make_low(pool, c + 2).then_inc(w_low_pool, 1)
                if s - 1 in POOL_ADDS:
                    add_halves(pool, s - 1).then_inc(added_pool, 1)
            if STEPS - 1 in POOL_ADDS:
                add_halves(pool, STEPS - 1).then_inc(added_pool, 1)

        @block.scalar
        def _(act):
            def high_weights(c):
                s = c % W_SLOTS
                act.wait_ge(w_loaded[c % RAW_SLOTS], 32 * (c // RAW_SLOTS + 1))
                if c >= W_SLOTS:
                    act.wait_ge(y_ready, CHUNK // 2 * (c - W_SLOTS + 1))
                act.activation(w_high[:, s, :], w_raw[:, c % RAW_SLOTS, :], ACT.Copy).then_inc(w_high_made, 1)

            def high_rows(g, half):
                k = SPLIT_SEQ[(g, half)]
                wait_gathered(act, g, half)
                wait_parts_free(act, k)
                act.activation(parts[:, k % 2, :, :, 0:D].bitcast(F32R), rows_of(g, half),
                               ACT.Copy).then_inc(rows_high, 1)

            def copy_turn(turn):
                act.wait_ge(turned, TURN_SEQ[turn] + 1)
                if turn[0] == "x":
                    act.activation(x_mov[:, turn[1], :], t_ps[:], ACT.Copy).then_inc(turn_copied, 1)
                    return
                _, g, kind = turn
                if g >= 2:
                    act.wait_ge(prod_ready, LAST_STEP_OF_LEAVES[g - 2] + 1)
                if kind in (AB, BC):
                    h = slice(0, D) if kind == AB else slice(D, P)
                    ins = act.activation(x_leaf[h, g % 2, LEAF_AT[AC], :], t_ps[h, :], ACT.Copy)
                if kind != AB or g < HALVED_GROUPS:
                    ins = act.activation(x_leaf[:, g % 2, LEAF_AT[kind], :], t_ps[:], ACT.Copy)
                ins.then_inc(turn_copied, 1)

            high_weights(0)
            high_weights(1)
            for s in range(STEPS):
                if s % (CHUNK // 2) == 0 and s // (CHUNK // 2) + 2 < CHUNKS:
                    high_weights(s // (CHUNK // 2) + 2)
                for job in JOBS_AT[s]:
                    if job[0] == "split":
                        high_rows(*job[1:])
                    else:
                        copy_turn(job)
                if (r := round_at(s)) is not None and r % BANK_ROUNDS == BANK_ROUNDS - 1:
                    act.wait_ge(round_summed, r + 1)
                    act.activation(z_sb[:, r // BANK_ROUNDS, :], z_ps[:], ACT.Copy).then_inc(z_saved, 1)
            act.wait_ge(round_summed, ROUNDS)
            act.wait_ge(dense_loaded, 16)
            for c in range(LAST_UNITS):
                act.activation(z_sb[32 * c:32 * c + 4, BANKS - 1, :], z_ps[32 * c:32 * c + 4, :],
                               ACT.Copy).then_inc(z_saved, 1)
            act.wait_ge(mlp_loaded, 64)
            for m in range(M1):
                act.wait_ge(h1_summed, m + 1)
                act.activation(h1_sb[:, m, :], h1_ps[m], ACT.Relu, bias=b1_sb[:, m:m + 1]).then_inc(h1_ready, 1)
            for m in range(M2):
                act.wait_ge(h2_summed, m + 1)
                act.activation(h2_sb[:, m, :], h2_ps[m], ACT.Relu, bias=b2_sb[:, m:m + 1]).then_inc(h2_ready, 1)
            act.wait_ge(out_summed, 1)
            act.activation(y_sb, out_ps, ACT.Copy).then_inc(out_ready, 1)

        @block.vector
        def _(dve):
            dve.memset(selector2[:], 0.0).then_inc(selector_zeroed, 1)
            dve.memset(selector4[:], 0.0).then_inc(selector_zeroed, 1)
            dve.memset(z_sb[:, BANKS - 1, :], 0.0).then_inc(z_zeroed, 1)
            dve.wait_ge(selector_zeroed, 2)
            for n in range(2):
                dve.memset(selector2[D * n:D * n + D, 30 + n:31 + n], 1.0).then_inc(selector_ready, 1)
            for n in range(4):
                dve.memset(selector4[32 * n:32 * n + 32, 28 + n:29 + n], 1.0).then_inc(selector_ready, 1)

            def low_rows(g, half):
                k = SPLIT_SEQ[(g, half)]
                dve.wait_ge(rows_high, k + 1)
                wait_parts_free(dve, k)
                dve.tensor_tensor(parts[:, k % 2, :, :, D:2 * D], rows_of(g, half),
                                  parts[:, k % 2, :, :, 0:D], ALU.subtract).then_inc(rows_low, 1)

            def multiply(s):
                dve.wait_ge(y_ready, s + 1)
                if s >= G_UNITS:
                    dve.wait_ge(round_summed, (s - G_UNITS) // ROUND + 1)
                (_, g0, kind0), (_, g1, kind1) = UNITS[s]
                for g, kind in ((g0, kind0), (g1, kind1)):
                    dve.wait_ge(turn_copied, turns_until(("leaves", g, kind)))
                at = 2 * (s % G_UNITS)
                if kind0 == EVEN or (g0, kind0) == (g1, kind1):
                    if kind0 == EVEN:
                        both = x_leaf[:, g0 % 2, LEAF_AT[EVEN]:LEAF_AT[ODD] + 1, :]
                    else:
                        both = x_leaf[:, g0 % 2, LEAF_AT[kind0]:LEAF_AT[kind0] + 1, :].to_broadcast([P, 2, B])
                    ins = dve.tensor_tensor(prod[:, at:at + 2, :], y_ps[:, s % Y_SLOTS], both, ALU.mult)
                else:
                    for n, (g, kind) in enumerate(((g0, kind0), (g1, kind1))):
                        ins = dve.tensor_tensor(prod[:, at + n, :], y_ps[:, s % Y_SLOTS, n, :],
                                                x_leaf[:, g % 2, LEAF_AT[kind], :], ALU.mult)
                ins.then_inc(prod_ready, 1)

            for c in range(2):
                make_low(dve, c).then_inc(w_low_made, 1)
            for s in range(STEPS):
                c = s // (CHUNK // 2) + 2
                if s % (CHUNK // 2) == 0 and c < POOL_SPLITS_FROM:
                    make_low(dve, c).then_inc(w_low_made, 1)
                for job in JOBS_AT[s]:
                    if job[0] == "split":
                        low_rows(*job[1:])
                multiply(s)
                if s - 1 in DVE_ADDS:
                    add_halves(dve, s - 1).then_inc(added_dve, 1)
            if STEPS - 1 in DVE_ADDS:
                add_halves(dve, STEPS - 1).then_inc(added_dve, 1)

        @block.tensor
        def _(pe):
            def turn(what):
                k = TURN_SEQ[what]
                if k:
                    pe.wait_ge(turn_copied, k)
                if what[0] == "x":
                    g, f = divmod(what[1], GF)
                    split = SPLIT_SEQ[(g, f // 2)]
                    pe.wait_ge(rows_low, split + 1)
                    src = [parts[:, split % 2, bt, f % 2, :] for bt in range(BT)]
                else:
                    _, g, kind = what
                    cols = (slice(kind - EVEN, GF * D, 2) if kind not in FIELDS_OF else
                            slice(FIELDS_OF[kind][0] * D, FIELDS_OF[kind][1] * D + D))
                    wait_gathered(pe, g, 0)
                    if kind != AB:
                        wait_gathered(pe, g, 1)
                    src = [rows[:, g % ROW_SLOTS, bt, cols] for bt in range(BT)]
                for bt in range(BT):
                    ins = pe.transpose(t_ps[:, P * bt:P * bt + P], src[bt], ident[:])
                ins.then_inc(turned, 1)

            def tiles(s):
                c = 2 * s // CHUNK
                if s % (CHUNK // 2) == 0:
                    pe.wait_ge(w_high_made, c + 1)
                    wait_low(pe, c)
                if s >= Y_SLOTS:
                    pe.wait_ge(prod_ready, s - Y_SLOTS + 1)
                for n, (mover, _, _) in enumerate(UNITS[s]):
                    pe.wait_ge(turn_copied, turns_until(("x", mover)))
                    at = P * ((2 * s + n) % CHUNK)
                    for k, w in enumerate((w_high, w_low)):
                        ins = pe.matmul(y_ps[:, s % Y_SLOTS, n, :], w[:, c % W_SLOTS, at:at + P],
                                        x_mov[:, mover, :], start=(k == 0), stop=(k == 1))
                ins.then_inc(y_ready, 1)

            def sum_round(r):
                units = range(ROUND * r, min(ROUND * r + ROUND, STEPS))
                pe.wait_ge(prod_ready, units[-1] + 1)
                for adds, added in ((DVE_ADDS, added_dve), (POOL_ADDS, added_pool)):
                    if any(u in adds for u in units):
                        pe.wait_ge(added, sum(u <= units[-1] for u in adds))
                if r == 0:
                    pe.wait_ge(selector_ready, 6)
                elif r % BANK_ROUNDS == 0:
                    pe.wait_ge(z_saved, r // BANK_ROUNDS)
                row = 4 * (r % BANK_ROUNDS)
                for n in range(2):
                    for u in units:
                        alone = u in DVE_ADDS or u in POOL_ADDS
                        if n and alone:
                            continue
                        if UNITS[u][n][2] == EVEN + n:
                            select = selector4[:, 28 - row:60 - row]
                        else:
                            select = selector2[:, 30 - row - 2 * n:62 - row - 2 * n]
                        last = (n or alone) and (r % BANK_ROUNDS == BANK_ROUNDS - 1 or u + ROUND >= STEPS)
                        q = 32 * (u % ROUND)
                        ins = pe.matmul(z_ps[q:q + 32, :], select, prod[:, 2 * (u % G_UNITS) + n, :],
                                        start=(n == 0 and row == 0), stop=bool(last))
                ins.then_inc(round_summed, 1)

            pe.wait_ge(ident_ready, 1)
            for s in range(STEPS):
                for job in JOBS_AT[s]:
                    if job[0] != "split":
                        turn(job)
                tiles(s)
                if (r := round_at(s)) is not None:
                    sum_round(r)
            for r in range(ROUNDS):
                if ROUND * r + ROUND - 1 + SUM_LAG >= STEPS:
                    sum_round(r)

            pe.wait_ge(mlp_loaded, 64)
            pe.wait_ge(w1_loaded, 16)
            pe.wait_ge(prod_ready, STEPS)
            for b in range(BANKS):
                pe.wait_ge(z_saved, b + 1 if b < BANKS - 1 else b + LAST_UNITS)
                for m in range(M1):
                    ins = pe.matmul(h1_ps[m], w1_sb[:, b, P * m:P * m + P], z_sb[:, b, :],
                                    start=(b == 0), stop=(b == BANKS - 1))
                    if b == BANKS - 1:
                        ins.then_inc(h1_summed, 1)
            for k in range(M1):
                pe.wait_ge(h1_ready, k + 1)
                for m in range(M2):
                    ins = pe.matmul(h2_ps[m], w2_sb[:, k, P * m:P * m + P], h1_sb[:, k, :],
                                    start=(k == 0), stop=(k == M1 - 1))
                    if k == M1 - 1:
                        ins.then_inc(h2_summed, 1)
            for k in range(M2):
                pe.wait_ge(h2_ready, k + 1)
                ins = pe.matmul(out_ps, w3_sb[:, k:k + 1], h2_sb[:, k, :], start=(k == 0), stop=(k == M2 - 1))
            ins.then_inc(out_summed, 1)


def pair_numbers():
    return {p: n for n, p in enumerate(zip(*np.triu_indices(F, k=1)))}


def lay_out_pairs(w):
    number = pair_numbers()
    laid = np.zeros((CHUNKS, D, CHUNK, P), w.dtype)
    for t in range(NT):
        for i, j, rows, elements, _ in pairs_of(t):
            m = w[number[(i, j)]] if i < j else w[number[(j, i)]].T
            laid[t // CHUNK, :, t % CHUNK, rows] = m[:, elements]
    return laid.reshape(CHUNKS, D, CHUNK * P)


def lay_out_top1(w):
    number = pair_numbers()
    laid = np.zeros((P, BANKS, N1), w.dtype)
    for t in range(NT):
        for i, j, _, _, n in pairs_of(t):
            bank, row = z_row(t // 2, n)
            laid[row, bank] = w[number[(min(i, j), max(i, j))]]
    laid[DENSE_ROW:DENSE_ROW + N_DENSE, BANKS - 1] = w[len(number):]
    return laid


def kernel(**inputs):
    import concourse.bacc as _bacc
    from concourse.bass_utils import run_bass_kernel_spmd as _run

    a = {name: np.ascontiguousarray(x) for name, x in inputs.items()}
    arrays = {
        "in_ids": a["ids"],
        **{f"in_tbl_{f}": a[f"tbl_{f}"] for f in range(F)},
        "in_dense_t": np.ascontiguousarray(a["dense_ctx"].T),
        "in_w_pairs": lay_out_pairs(a["L0_rec_W"]),
        "in_w1": lay_out_top1(a["W_top1"]),
        "in_b1": np.ascontiguousarray(a["b_top1"].reshape(M1, P).T),
        "in_w2": np.ascontiguousarray(a["W_top2"].reshape(M1, P, N2).transpose(1, 0, 2)),
        "in_b2": np.ascontiguousarray(a["b_top2"].reshape(M2, P).T),
        "in_w3": np.ascontiguousarray(a["W_top3"].reshape(M2, P).T),
    }
    nc = _bacc.Bacc("TRN2", target_bir_lowering=False, num_devices=1)
    ap = {name: nc.dram_tensor(name, x.shape, mybir.dt.from_np(x.dtype), kind="ExternalInput").ap()
          for name, x in arrays.items()}
    out = nc.dram_tensor("out_y", (B, 1), F32, kind="ExternalOutput").ap()
    dlrm_tower(nc, ap["in_ids"], [ap[f"in_tbl_{f}"] for f in range(F)], ap["in_dense_t"], ap["in_w_pairs"],
               ap["in_w1"], ap["in_b1"], ap["in_w2"], ap["in_b2"], ap["in_w3"], out)
    r = _run(nc, [arrays], core_ids=[0])
    return r.results[0]["out_y"]
```

```python
from contextlib import ExitStack

import numpy as np

import concourse.bass as bass
from concourse import mybir

ALU = mybir.AluOpType
ACT = mybir.ActivationFunctionType
F32 = mybir.dt.float32
F32R = mybir.dt.float32r
I32 = mybir.dt.int32

P = 128
B = 512
BT = B // P
F = 40
D = 64
GF = 4
NG = F // GF
N_DENSE = 16
N1, N2 = 512, 256
M1, M2 = N1 // P, N2 // P

AB, CD, BC, AC, EVEN, ODD = range(6)
FIELDS_OF = {AB: (0, 1), CD: (2, 3), BC: (1, 2), AC: (0, 2)}
LEAF_AT = {AB: 0, EVEN: 0, ODD: 1, CD: 2, BC: 3, AC: 4}
N_LEAF = 5

CHUNK = 8
RAW_SLOTS = 2
W_SLOTS = 3
Y_SLOTS = 3
G_UNITS = 8
ROW_SLOTS = 4
ROUND = 4
BANK_ROUNDS = 8
SUM_LAG = 3

ONE_HOT_GROUPS = (1,)
ONE_HOT_FIELDS = (0, 1, 3, 4)
TABLE_ROWS = 1000
TP = 125
TK = TABLE_ROWS // TP

HALVED_GROUPS = 4
INNER_AFTER = 10
LEAF_LEAD = 3
W1_AFTER = 6
PARTIAL_PAIRS = 2
PARTIAL_EVERY = 8
SPLIT_AT = (3, 4, 6, 8)
POOL_SPLITS_FROM = 20
ADDED_ROUNDS = [r for r in range(18, 49) if r % 4]
POOL_TURNS = (0, 1, 2)


def plan_order():
    one_hot, others = list(ONE_HOT_FIELDS), [f for f in range(F) if f not in ONE_HOT_FIELDS]
    return [(one_hot if p // GF in ONE_HOT_GROUPS else others).pop(0) for p in range(F)]


ORDER = plan_order()
GATHERED = [g for g in range(NG) if g not in ONE_HOT_GROUPS]


def plan_units():
    units, first, first_cd = [], [], []
    for g in range(NG):
        a, movers = GF * g, range(GF * g)
        first.append(len(units))
        inner = [((a - 1, g - 1, AC), (a + 3, g, AC))] if g % 2 else []
        inner.append(((a + 1, g, CD), (a, g, BC)))
        if g < HALVED_GROUPS:
            units += [((i, g, AB), (i + 1, g, AB)) for i in movers[::2]]
            first_cd.append(len(units))
            cross = [((i, g, CD), (i + 1, g, CD)) for i in movers[::2]]
            after = len(cross) if g + 1 < HALVED_GROUPS else len(cross) - LEAF_LEAD
        else:
            first_cd.append(len(units))
            cross = [((i, g, EVEN), (i, g, ODD)) for i in movers]
            after = INNER_AFTER
        units += cross[:after] + inner + cross[after:]
    return units, first, first_cd


UNITS, FIRST_AB, FIRST_CD = plan_units()
STEPS = len(UNITS)
TILES = [tile for unit in UNITS for tile in unit]
NT = len(TILES)
CHUNKS = -(-NT // CHUNK)
ROUNDS = -(-STEPS // ROUND)
BANKS = -(-ROUNDS // BANK_ROUNDS)
LAST_UNITS = STEPS - ROUND * BANK_ROUNDS * (BANKS - 1)
assert LAST_UNITS <= ROUND
FIRST_LATE = 2 * PARTIAL_PAIRS
DENSE_ROW = 4


ADDS = [u for u in range(STEPS) if u // ROUND in ADDED_ROUNDS and UNITS[u][0][2] == EVEN]
POOL_ADDS = [u for u in ADDS if u % ROUND in POOL_TURNS]
DVE_ADDS = [u for u in ADDS if u % ROUND not in POOL_TURNS]


def pairs_of(t):
    mover, g, kind = TILES[t]
    if kind in FIELDS_OF:
        return [(mover, GF * g + f, slice(D * n, D * n + D), slice(0, D), 2 * (t % 2) + n)
                for n, f in enumerate(FIELDS_OF[kind])]
    return [(mover, GF * g + f, slice(D // 2 * f, D // 2 * (f + 1)), slice(kind - EVEN, D, 2), f)
            for f in range(GF)]


def z_row(u, n):
    r = u // ROUND
    return r // BANK_ROUNDS, 32 * (u % ROUND) + 4 * (r % BANK_ROUNDS) + n


FIRST_JOBS = [
    (0, ("one_hot", 4)), (0, ("one_hot", 5)), (0, ("weights", 0)), (0, ("x", 4)), (0, ("one_hot", 6)),
    (0, ("leaves", 0, AB)), (0, ("split", 0)), (0, ("split", 1)), (0, ("x", 5)), (0, ("one_hot", 7)),
    (0, ("leaves", 1, AB)), (0, ("x", 6)), (0, ("leaves", 0, CD)), (0, ("leaves", 0, BC)),
    (0, ("split", 3)), (0, ("split", 2)), (0, ("weights", 1)),
    (1, ("x", 7)), (2, ("leaves", 1, CD)), (4, ("leaves", 1, BC))]


TURNS = ("x", "leaves", "partial")
W1_PAIRS = -(-BANKS // 2)


def plan_jobs():
    jobs_at = [[] for _ in range(STEPS)]
    for g in range(NG):
        a, f, cd = GF * g, FIRST_AB[g], FIRST_CD[g]
        if g in ONE_HOT_GROUPS:
            continue
        if g == 0:
            jobs = FIRST_JOBS
        elif g < HALVED_GROUPS:
            jobs = [(f, ("leaves", g, AB)), (f + 1, ("split", a)), (f + 2, ("split", a + 1)),
                    (cd, ("leaves", g, CD)), (cd + 1, ("split", a + 3)), (cd + 2, ("leaves", g, BC)),
                    (cd + 3, ("split", a + 2))]
        else:
            turns = [("leaves", g, kind) for kind in (EVEN, ODD, AB, BC, CD)]
            jobs = [(f - LEAF_LEAD + n, turn) for n, turn in enumerate(turns)]
            jobs += [(f + at, ("split", a + n)) for n, at in enumerate(SPLIT_AT)]
        for at, job in jobs:
            jobs_at[min(at, needed(job))].append(job)
    for c in range(2, CHUNKS):
        jobs_at[max(1, CHUNK // 2 * (c - 2))].insert(0, ("weights", c))
    for pair in range(PARTIAL_PAIRS):
        group = GATHERED[len(GATHERED) - ROW_SLOTS + pair]
        turns_end = max(s for s, jobs in enumerate(jobs_at) for job in jobs if job[:2] == ("leaves", group))
        jobs_at[turns_end + W1_AFTER].append(("w1", pair))
        start = max(turns_end + W1_AFTER + 4, ROUND * BANK_ROUNDS * 2 * (pair + 1) + SUM_LAG + 1)
        for m in range(M1):
            jobs_at[start + PARTIAL_EVERY * m].append(("partial", pair, m))
    return jobs_at


def needed(job):
    if job[0] == "one_hot":
        return STEPS
    uses = [s for s, unit in enumerate(UNITS) for i, g, kind in unit
            if job in (("x", i), ("split", i)) or job == ("leaves", g, kind)
            or (job[0] == "leaves" and job[1] == g and kind == AC and job[2] in (AB, BC))]
    return min(uses, default=STEPS)


JOBS_AT = plan_jobs()
JOBS = [job for at in JOBS_AT for job in at]
TURN_SEQ = {turn: n for n, turn in enumerate(j for j in JOBS if j[0] in TURNS)}
SPLIT_SEQ = {split[1]: n for n, split in enumerate(j for j in JOBS if j[0] == "split")}
EARLY_TURNS = sum(j[0] in TURNS for j in JOBS_AT[0])
TURN_BANK = [n % (2 * Y_SLOTS + 1) if n < EARLY_TURNS else 2 * Y_SLOTS for n in range(len(TURN_SEQ))]
ONE_HOTS = [j[1] for j in JOBS if j[0] == "one_hot"]


def turns_until(turn):
    if turn[0] == "leaves" and turn[2] == AC:
        turn = ("leaves", turn[1], BC)
    return TURN_SEQ[turn] + 1


def split_leaves_until(p):
    g, f = divmod(p, GF)
    kinds = (AB, AB, CD, CD) if g < HALVED_GROUPS else (AB, BC, CD, CD)
    return turns_until(("leaves", g, kinds[f]))


def group_turns_until(g):
    return 1 + max(n for t, n in TURN_SEQ.items() if t[0] != "partial" and (t[1] // GF if t[0] == "x" else t[1]) == g)


LAST_STEP_OF_LEAVES = [max(s for s, unit in enumerate(UNITS) if any(t[1] == g for t in unit))
                       for g in range(NG)]
for _s, _jobs in enumerate(JOBS_AT):
    for _t in _jobs:
        assert _t[0] != "leaves" or _t[1] < 2 or LAST_STEP_OF_LEAVES[_t[1] - 2] < _s, (_t, _s)


def dlrm_tower(nc, ids, ids_one_hot, row_numbers, tables, dense_t, w_pairs, w1, b1, w2, b2, w3, out):
    ctx = ExitStack()
    with ctx:
        def sb(name, shape, dt=F32):
            return ctx.enter_context(nc.sbuf_tensor(name, shape, dt))

        def ps(name, shape):
            return ctx.enter_context(nc.psum_tensor(name, shape, F32))

        def sem(name):
            return ctx.enter_context(nc.semaphore(name))

        ids_sb = sb("ids_sb", [P, BT, F], I32)
        ident = sb("ident", [P, P])
        selector2 = sb("selector2", [P, 62])
        selector4 = sb("selector4", [P, 60])
        rows = sb("rows", [P, ROW_SLOTS, BT, GF * D])
        x_mov = sb("x_mov", [P, F, B], F32R)
        x_leaf = sb("x_leaf", [P, 2, N_LEAF, B])
        fold = sb("fold", [P, 3 * D], F32R)
        numbers = sb("numbers", [TP, TK])
        w_raw = sb("w_raw", [P, RAW_SLOTS, CHUNK * P])
        w_high = sb("w_high", [P, W_SLOTS, CHUNK * P], F32R)
        w_low = sb("w_low", [P, W_SLOTS, CHUNK * P], F32R)
        prod = sb("prod", [P, 2 * G_UNITS, B])
        z_sb = sb("z_sb", [P, BANKS, B])
        w2_sb = sb("w2_sb", [P, M1, N2])
        partial_sb = sb("partial_sb", [P, M1 - 1, B])
        w3_sb = sb("w3_sb", [P, M2])
        b1_sb = sb("b1_sb", [P, M1])
        b2_sb = sb("b2_sb", [P, M2])
        early = z_sb[0:TP, 0:4, :].rearrange("p b n -> p (b n)")
        ids_all = early[:, 0:2 * B].bitcast(I32).rearrange("p (s n) -> p s n", s=2)
        table = early[:, 2 * B:4 * B].rearrange("p (s n) -> p s n", s=2)
        spare = x_mov[0:TP, F - 20:F, :].rearrange("p f b -> p (f b)")
        table_parts = spare[:, 0:4 * B].rearrange("p (s k n) -> p s k n", s=2, n=2 * D)
        one_hot = spare[:, 4 * B:20 * B].rearrange("p (s k n) -> p s k n", s=2, n=B)
        w1_sb = [rows[:, (len(GATHERED) + b // 2) % ROW_SLOTS].rearrange("p t n -> p (t n)")[
            :, N1 * (b % 2):N1 * (b % 2) + N1] for b in range(BANKS)]
        partial = [partial_sb[:, m, :] for m in range(M1 - 1)] + [z_sb[:, 0, :]]
        h1_sb = prod[:, 0:M1, :]
        h2_sb = prod[:, M1:M1 + M2, :]
        y_sb = prod[0:1, M1 + M2, :]

        y_ps = ps("y_ps", [P, Y_SLOTS, 2, B])
        z_ps = ps("z_ps", [P, B])
        t_ps = ps("t_ps", [P, B])[:]

        def turn_ps(n):
            bank = TURN_BANK[n]
            return t_ps if bank == 2 * Y_SLOTS else y_ps[:, bank // 2, bank % 2, :]

        h1_ps = [y_ps[:, m // 2, m % 2, :] for m in range(M1)]
        h2_ps = [y_ps[:, 2, m, :] for m in range(M2)]
        out_ps = t_ps[0:1, :]

        ids_loaded = sem("ids_loaded")
        gathered = [[sem(f"gathered{s}_{h}") for h in range(2)] for s in range(ROW_SLOTS)]
        w_loaded = [sem(f"w_loaded{s}") for s in range(RAW_SLOTS)]
        table_loaded = [sem(f"table_loaded{s}") for s in range(2)]
        numbers_loaded = sem("numbers_loaded")
        w1_loaded = [sem(f"w1_loaded{n}") for n in range(W1_PAIRS)]
        mlp_loaded = sem("mlp_loaded")
        dense_loaded = sem("dense_loaded")
        ident_zeroed = sem("ident_zeroed")
        ident_ready = sem("ident_ready")
        fold_zeroed = sem("fold_zeroed")
        fold_ready = sem("fold_ready")
        table_high = sem("table_high")
        one_hot_made = sem("one_hot_made")
        selector_zeroed = sem("selector_zeroed")
        selector_ready = sem("selector_ready")
        z_zeroed = sem("z_zeroed")
        mover_high = sem("mover_high")
        mover_low = sem("mover_low")
        w_high_made = sem("w_high_made")
        w_low_made = sem("w_low_made")
        w_low_pool = sem("w_low_pool")
        turned = sem("turned")
        turn_copied = sem("turn_copied")
        y_ready = sem("y_ready")
        prod_ready = sem("prod_ready")
        added_dve = sem("added_dve")
        added_pool = sem("added_pool")
        round_summed = sem("round_summed")
        z_saved = sem("z_saved")
        h1_summed = sem("h1_summed")
        h1_added = sem("h1_added")
        h1_ready = sem("h1_ready")
        h2_summed = sem("h2_summed")
        h2_ready = sem("h2_ready")
        out_summed = sem("out_summed")
        out_ready = sem("out_ready")
        out_stored = sem("out_stored")

        def wait_low(eng, c):
            if c < POOL_SPLITS_FROM:
                eng.wait_ge(w_low_made, c + 1)
            else:
                eng.wait_ge(w_low_pool, c + 1 - POOL_SPLITS_FROM)

        def make_low(eng, c):
            s = c % W_SLOTS
            eng.wait_ge(w_high_made, c + 1)
            if c >= W_SLOTS:
                eng.wait_ge(y_ready, CHUNK // 2 * (c - W_SLOTS + 1))
            return eng.tensor_tensor(w_low[:, s, :], w_raw[:, c % RAW_SLOTS, :], w_high[:, s, :].bitcast(F32),
                                     ALU.subtract)

        def wait_gathered(eng, g, half):
            turn, slot = divmod(GATHERED.index(g), ROW_SLOTS)
            eng.wait_ge(gathered[slot][half], 16 * 2 * BT * (turn + 1))

        def mover_parts(p):
            g, f = divmod(p, GF)
            if g < HALVED_GROUPS:
                kind, half = (AB, AB, CD, CD)[f], f % 2
            else:
                kind, half = (AC, BC, CD, CD)[f], f // 3
            own, other = (slice(0, D), slice(D, P))[::1 - 2 * half]
            return x_leaf[own, g % 2, LEAF_AT[kind], :], x_mov[own, p, :], x_mov[other, p, :]

        def wait_mover(eng, p):
            if p in SPLIT_SEQ:
                eng.wait_ge(mover_low, SPLIT_SEQ[p] + 1)
            else:
                eng.wait_ge(turn_copied, turns_until(("x", p)))

        def round_at(s):
            r, rest = divmod(s - SUM_LAG - (ROUND - 1), ROUND)
            return r if rest == 0 and r >= 0 else None

        def add_halves(eng, u):
            at = 2 * (u % G_UNITS)
            eng.wait_ge(prod_ready, u + 1)
            return eng.tensor_tensor(prod[:, at, :], prod[:, at, :], prod[:, at + 1, :], ALU.add)

        block = ctx.enter_context(nc.Block())

        @block.sync
        def _(sp):
            sp.dma_start(ids_sb[:], ids.rearrange("(t p) f -> p t f", p=P)).then_inc(ids_loaded, 16)
            sp.dma_start(numbers[:], row_numbers).then_inc(numbers_loaded, 16)
            def load_w1(pair):
                sp.wait_ge(turned, group_turns_until(GATHERED[len(GATHERED) - ROW_SLOTS + pair]))
                for b in range(2 * pair, min(2 * pair + 2, BANKS)):
                    sp.dma_start(w1_sb[b], w1[:, b, :]).then_inc(w1_loaded[pair], 16)

            for kind, c in [job for job in JOBS if job[0] in ("one_hot", "weights", "w1")]:
                if kind == "w1":
                    load_w1(c)
                    continue
                if kind == "one_hot":
                    n = ONE_HOTS.index(c)
                    if n >= 2:
                        sp.wait_ge(one_hot_made, 2 * (n - 1))
                    sp.dma_start(ids_all[:, n % 2, :],
                                 ids_one_hot[n:n + 1, :].to_broadcast([TP, B])).then_inc(table_loaded[n % 2], 16)
                    sp.dma_start(table[:, n % 2, :], tables[ORDER[c]].rearrange(
                        "(p k) d -> p (k d)", k=TK)).then_inc(table_loaded[n % 2], 16)
                    continue
                if c >= RAW_SLOTS:
                    wait_low(sp, c - RAW_SLOTS)
                for half in range(2):
                    sp.dma_start(w_raw[D * half:D * half + D, c % RAW_SLOTS, :],
                                 w_pairs[c]).then_inc(w_loaded[c % RAW_SLOTS], 16)
                if c == 6:
                    sp.wait_ge(z_zeroed, 1)
                    sp.dma_start(z_sb[DENSE_ROW:DENSE_ROW + N_DENSE, BANKS - 1, :],
                                 dense_t).then_inc(dense_loaded, 16)
                if c == 12:
                    sp.dma_start(w2_sb[:], w2).then_inc(mlp_loaded, 16)
                    sp.dma_start(w3_sb[:], w3).then_inc(mlp_loaded, 16)
                    sp.dma_start(b1_sb[:], b1).then_inc(mlp_loaded, 16)
                    sp.dma_start(b2_sb[:], b2).then_inc(mlp_loaded, 16)
            for pair in range(PARTIAL_PAIRS, W1_PAIRS):
                load_w1(pair)
            sp.wait_ge(out_ready, 1)
            sp.dma_start(out.rearrange("b o -> o b"), y_sb).then_inc(out_stored, 16)
            sp.wait_ge(out_stored, 16)

        @block.gpsimd
        def _(pool):
            pool.memset(ident[:], 0.0).then_inc(ident_zeroed, 1)
            pool.wait_ge(ident_zeroed, 1)
            pool.affine_select(out=ident[:], in_=ident[:], compare_op=ALU.not_equal, fill=1.0, base=0,
                               pattern=[[-1, P]], channel_multiplier=1).then_inc(ident_ready, 1)
            pool.wait_ge(ids_loaded, 16)
            for n, g in enumerate(GATHERED):
                if n >= ROW_SLOTS:
                    pool.wait_ge(turned, group_turns_until(GATHERED[n - ROW_SLOTS]))
                for f in range(GF):
                    for bt in range(BT):
                        pool.indirect_dma_start(
                            rows[:, n % ROW_SLOTS, bt, f * D:(f + 1) * D], None, tables[ORDER[GF * g + f]],
                            bass.IndirectOffsetOnAxis(
                                ap=ids_sb[:, bt, ORDER[GF * g + f]:ORDER[GF * g + f] + 1], axis=0),
                        ).then_inc(gathered[n % ROW_SLOTS][f // 2], 16)
            for s in range(STEPS):
                for job in JOBS_AT[s]:
                    if job[0] == "weights" and job[1] >= POOL_SPLITS_FROM:
                        make_low(pool, job[1]).then_inc(w_low_pool, 1)
                if s - 1 in POOL_ADDS:
                    add_halves(pool, s - 1).then_inc(added_pool, 1)
            if STEPS - 1 in POOL_ADDS:
                add_halves(pool, STEPS - 1).then_inc(added_pool, 1)

        @block.scalar
        def _(act):
            def high_weights(c):
                s = c % W_SLOTS
                act.wait_ge(w_loaded[c % RAW_SLOTS], 32 * (c // RAW_SLOTS + 1))
                if c >= W_SLOTS:
                    act.wait_ge(y_ready, CHUNK // 2 * (c - W_SLOTS + 1))
                act.activation(w_high[:, s, :], w_raw[:, c % RAW_SLOTS, :], ACT.Copy).then_inc(w_high_made, 1)

            def high_mover(p):
                leaf, high, _ = mover_parts(p)
                act.wait_ge(turn_copied, split_leaves_until(p))
                act.activation(high, leaf, ACT.Copy).then_inc(mover_high, 1)

            def copy_turn(turn):
                act.wait_ge(turned, TURN_SEQ[turn] + 1)
                src = turn_ps(TURN_SEQ[turn])
                if turn[0] == "x":
                    act.activation(x_mov[:, turn[1], :], src[:], ACT.Copy).then_inc(turn_copied, 1)
                    return
                if turn[0] == "partial":
                    if turn[1] == 0:
                        act.activation(partial[turn[2]], src[:], ACT.Copy).then_inc(turn_copied, 1)
                    return
                _, g, kind = turn
                if g >= 2:
                    act.wait_ge(prod_ready, LAST_STEP_OF_LEAVES[g - 2] + 1)
                if kind in (AB, BC):
                    h = slice(0, D) if kind == AB else slice(D, P)
                    ins = act.activation(x_leaf[h, g % 2, LEAF_AT[AC], :], src[h, :], ACT.Copy)
                if kind != AB or g < HALVED_GROUPS:
                    ins = act.activation(x_leaf[:, g % 2, LEAF_AT[kind], :], src[:], ACT.Copy)
                ins.then_inc(turn_copied, 1)

            def save_bank(r):
                act.wait_ge(round_summed, r + 1)
                act.activation(z_sb[:, r // BANK_ROUNDS, :], z_ps[:], ACT.Copy).then_inc(z_saved, 1)

            def high_table(p):
                n = ONE_HOTS.index(p)
                act.wait_ge(table_loaded[n % 2], 32 * (n // 2 + 1))
                if n >= 2:
                    act.wait_ge(turned, turns_until(("x", ONE_HOTS[n - 2])))
                act.activation(table_parts[:, n % 2, :, 0:D], table[:, n % 2, :].rearrange("p (k d) -> p k d", d=D),
                               ACT.Copy).then_inc(table_high, 1)

            for s in range(STEPS):
                for job in JOBS_AT[s]:
                    if job[0] == "weights":
                        high_weights(job[1])
                    elif job[0] == "one_hot":
                        high_table(job[1])
                    elif job[0] == "split":
                        high_mover(job[1])
                    elif job[0] in TURNS:
                        copy_turn(job)
                if (r := round_at(s)) is not None and r % BANK_ROUNDS == BANK_ROUNDS - 1:
                    save_bank(r)
            for r in range(BANK_ROUNDS - 1, ROUNDS, BANK_ROUNDS):
                if ROUND * r + ROUND - 1 + SUM_LAG >= STEPS:
                    save_bank(r)
            act.wait_ge(round_summed, ROUNDS)
            act.wait_ge(dense_loaded, 16)
            for c in range(LAST_UNITS):
                act.activation(z_sb[32 * c:32 * c + 4, BANKS - 1, :], z_ps[32 * c:32 * c + 4, :],
                               ACT.Copy).then_inc(z_saved, 1)
            act.wait_ge(mlp_loaded, 64)
            for m in range(M1):
                act.wait_ge(h1_added, m + 1)
                act.activation(h1_sb[:, m, :], partial[m], ACT.Relu, bias=b1_sb[:, m:m + 1]).then_inc(h1_ready, 1)
            for m in range(M2):
                act.wait_ge(h2_summed, m + 1)
                act.activation(h2_sb[:, m, :], h2_ps[m], ACT.Relu, bias=b2_sb[:, m:m + 1]).then_inc(h2_ready, 1)
            act.wait_ge(out_summed, 1)
            act.activation(y_sb, out_ps, ACT.Copy).then_inc(out_ready, 1)

        @block.vector
        def _(dve):
            dve.memset(selector2[:], 0.0).then_inc(selector_zeroed, 1)
            dve.memset(selector4[:], 0.0).then_inc(selector_zeroed, 1)
            dve.memset(z_sb[:, BANKS - 1, :], 0.0).then_inc(z_zeroed, 1)
            dve.wait_ge(selector_zeroed, 2)
            for n in range(2):
                dve.memset(selector2[D * n:D * n + D, 30 + n:31 + n], 1.0).then_inc(selector_ready, 1)
            for n in range(4):
                dve.memset(selector4[32 * n:32 * n + 32, 28 + n:29 + n], 1.0).then_inc(selector_ready, 1)

            dve.memset(fold[:].bitcast(F32), 0.0).then_inc(fold_zeroed, 1)
            dve.wait_ge(fold_zeroed, 1)
            dve.wait_ge(ident_ready, 1)
            dve.tensor_tensor(fold[:, D:2 * D], ident[:, 0:D], ident[:, D:P], ALU.add).then_inc(fold_ready, 1)

            def compare_ids(p):
                n = ONE_HOTS.index(p)
                dve.wait_ge(table_high, n + 1)
                dve.tensor_tensor(table_parts[:, n % 2, :, D:P],
                                  table[:, n % 2, :].rearrange("p (k d) -> p k d", d=D),
                                  table_parts[:, n % 2, :, 0:D].bitcast(F32), ALU.subtract)
                if n == 0:
                    dve.wait_ge(numbers_loaded, 16)
                if n >= 2:
                    dve.wait_ge(turned, turns_until(("x", ONE_HOTS[n - 2])))
                for k in range(TK):
                    ins = dve.tensor_scalar(one_hot[:, n % 2, k, :], ids_all[:, n % 2, :],
                                            numbers[:, k:k + 1], None, ALU.is_equal)
                    if k % (TK // 2) == TK // 2 - 1:
                        ins.then_inc(one_hot_made, 1)

            def low_mover(p):
                leaf, high, low = mover_parts(p)
                dve.wait_ge(mover_high, SPLIT_SEQ[p] + 1)
                dve.tensor_tensor(low, leaf, high.bitcast(F32), ALU.subtract).then_inc(mover_low, 1)

            def add_partial(turn):
                k = TURN_SEQ[turn]
                dve.wait_ge(turned, k + 1)
                dve.tensor_tensor(partial[turn[2]], turn_ps(k), partial[turn[2]], ALU.add).then_inc(turn_copied, 1)

            def multiply(s):
                dve.wait_ge(y_ready, s + 1)
                if s >= G_UNITS:
                    dve.wait_ge(round_summed, (s - G_UNITS) // ROUND + 1)
                (_, g0, kind0), (_, g1, kind1) = UNITS[s]
                for g, kind in ((g0, kind0), (g1, kind1)):
                    dve.wait_ge(turn_copied, turns_until(("leaves", g, kind)))
                at = 2 * (s % G_UNITS)
                if kind0 == EVEN or (g0, kind0) == (g1, kind1):
                    if kind0 == EVEN:
                        both = x_leaf[:, g0 % 2, LEAF_AT[EVEN]:LEAF_AT[ODD] + 1, :]
                    else:
                        both = x_leaf[:, g0 % 2, LEAF_AT[kind0]:LEAF_AT[kind0] + 1, :].to_broadcast([P, 2, B])
                    ins = dve.tensor_tensor(prod[:, at:at + 2, :], y_ps[:, s % Y_SLOTS], both, ALU.mult)
                else:
                    for n, (g, kind) in enumerate(((g0, kind0), (g1, kind1))):
                        ins = dve.tensor_tensor(prod[:, at + n, :], y_ps[:, s % Y_SLOTS, n, :],
                                                x_leaf[:, g % 2, LEAF_AT[kind], :], ALU.mult)
                ins.then_inc(prod_ready, 1)

            for s in range(STEPS):
                for job in JOBS_AT[s]:
                    if job[0] == "weights" and job[1] < POOL_SPLITS_FROM:
                        make_low(dve, job[1]).then_inc(w_low_made, 1)
                    elif job[0] == "one_hot":
                        compare_ids(job[1])
                    elif job[0] == "split":
                        low_mover(job[1])
                    elif job[0] == "partial" and job[1]:
                        add_partial(job)
                multiply(s)
                if s in DVE_ADDS:
                    add_halves(dve, s).then_inc(added_dve, 1)

            for m in range(M1):
                dve.wait_ge(h1_summed, m + 1)
                dve.tensor_tensor(partial[m], h1_ps[m], partial[m], ALU.add).then_inc(h1_added, 1)

        @block.tensor
        def _(pe):
            def look_up(p, dst):
                n = ONE_HOTS.index(p)
                for k in range(TK):
                    if k % (TK // 2) == 0:
                        pe.wait_ge(one_hot_made, 2 * n + 1 + k // (TK // 2))
                    ins = pe.matmul(dst, table_parts[:, n % 2, k, :], one_hot[:, n % 2, k, :],
                                    start=(k == 0), stop=(k == TK - 1))
                ins.then_inc(turned, 1)

            def fold_leaves(g, kind, dst):
                pe.wait_ge(fold_ready, 1)
                for n, f in enumerate(FIELDS_OF[kind]):
                    pe.wait_ge(turn_copied, turns_until(("x", GF * g + f)))
                    ins = pe.matmul(dst, fold[:, D * (1 - n):D * (1 - n) + P], x_mov[:, GF * g + f, :],
                                    start=(n == 0), stop=(n == 1))
                ins.then_inc(turned, 1)

            def turn(what):
                k = TURN_SEQ[what]
                dst = turn_ps(k)
                if TURN_BANK[k] in TURN_BANK[:k]:
                    pe.wait_ge(turn_copied, max(n for n in range(k) if TURN_BANK[n] == TURN_BANK[k]) + 1)
                if what[0] == "x":
                    look_up(what[1], dst)
                    return
                if what[0] == "partial":
                    _, pair, m = what
                    pe.wait_ge(w1_loaded[pair], 32)
                    pe.wait_ge(z_saved, 2 * pair + 2)
                    for b in (2 * pair, 2 * pair + 1):
                        ins = pe.matmul(dst, w1_sb[b][:, P * m:P * m + P], z_sb[:, b, :],
                                        start=(b % 2 == 0), stop=(b % 2 == 1))
                    ins.then_inc(turned, 1)
                    return
                _, g, kind = what
                if g in ONE_HOT_GROUPS:
                    fold_leaves(g, kind, dst)
                    return
                cols = (slice(kind - EVEN, GF * D, 2) if kind not in FIELDS_OF else
                        slice(FIELDS_OF[kind][0] * D, FIELDS_OF[kind][1] * D + D))
                wait_gathered(pe, g, 0)
                if kind != AB:
                    wait_gathered(pe, g, 1)
                src = [rows[:, GATHERED.index(g) % ROW_SLOTS, bt, cols] for bt in range(BT)]
                for bt in range(BT):
                    ins = pe.transpose(dst[:, P * bt:P * bt + P], src[bt], ident[:])
                ins.then_inc(turned, 1)

            def tiles(s):
                c = 2 * s // CHUNK
                if s % (CHUNK // 2) == 0:
                    pe.wait_ge(w_high_made, c + 1)
                    wait_low(pe, c)
                if s >= Y_SLOTS:
                    pe.wait_ge(prod_ready, s - Y_SLOTS + 1)
                else:
                    pe.wait_ge(turn_copied, 1 + max(n for n, bank in enumerate(TURN_BANK) if bank // 2 == s))
                for n, (mover, _, _) in enumerate(UNITS[s]):
                    wait_mover(pe, mover)
                    at = P * ((2 * s + n) % CHUNK)
                    for k, w in enumerate((w_high, w_low)):
                        ins = pe.matmul(y_ps[:, s % Y_SLOTS, n, :], w[:, c % W_SLOTS, at:at + P],
                                        x_mov[:, mover, :], start=(k == 0), stop=(k == 1))
                ins.then_inc(y_ready, 1)

            def sum_round(r):
                units = range(ROUND * r, min(ROUND * r + ROUND, STEPS))
                pe.wait_ge(prod_ready, units[-1] + 1)
                for adds, added in ((DVE_ADDS, added_dve), (POOL_ADDS, added_pool)):
                    if any(u in adds for u in units):
                        pe.wait_ge(added, sum(u <= units[-1] for u in adds))
                if r == 0:
                    pe.wait_ge(selector_ready, 6)
                elif r % BANK_ROUNDS == 0:
                    pe.wait_ge(z_saved, r // BANK_ROUNDS)
                row = 4 * (r % BANK_ROUNDS)
                for n in range(2):
                    for u in units:
                        alone = u in DVE_ADDS or u in POOL_ADDS
                        if n and alone:
                            continue
                        if UNITS[u][n][2] == EVEN + n:
                            select = selector4[:, 28 - row:60 - row]
                        else:
                            select = selector2[:, 30 - row - 2 * n:62 - row - 2 * n]
                        last = (n or alone) and (r % BANK_ROUNDS == BANK_ROUNDS - 1 or u + ROUND >= STEPS)
                        q = 32 * (u % ROUND)
                        ins = pe.matmul(z_ps[q:q + 32, :], select, prod[:, 2 * (u % G_UNITS) + n, :],
                                        start=(n == 0 and row == 0), stop=bool(last))
                ins.then_inc(round_summed, 1)

            pe.wait_ge(ident_ready, 1)
            for s in range(STEPS):
                for job in JOBS_AT[s]:
                    if job[0] in TURNS:
                        turn(job)
                tiles(s)
                if (r := round_at(s)) is not None:
                    sum_round(r)
            def first_layer(b, m):
                if m == 0:
                    pe.wait_ge(w1_loaded[b // 2], 16 * (min(b | 1, BANKS - 1) % 2 + 1))
                    pe.wait_ge(z_saved, b + 1 if b < BANKS - 1 else b + LAST_UNITS)
                return pe.matmul(h1_ps[m], w1_sb[b][:, P * m:P * m + P], z_sb[:, b, :],
                                 start=(b == FIRST_LATE), stop=(b == BANKS - 1))

            for r in range(ROUNDS - 1):
                if ROUND * r + ROUND - 1 + SUM_LAG >= STEPS:
                    sum_round(r)
            assert (STEPS - LAST_UNITS) % Y_SLOTS == 0
            pe.wait_ge(prod_ready, STEPS - LAST_UNITS + 1)
            for m in range(2):
                first_layer(FIRST_LATE, m)
            sum_round(ROUNDS - 1)

            pe.wait_ge(prod_ready, STEPS)
            for b in range(FIRST_LATE, BANKS):
                for m in range(2 if b == FIRST_LATE else 0, M1):
                    ins = first_layer(b, m)
                    if b == BANKS - 1:
                        ins.then_inc(h1_summed, 1)
            pe.wait_ge(mlp_loaded, 64)
            for k in range(M1):
                pe.wait_ge(h1_ready, k + 1)
                for m in range(M2):
                    ins = pe.matmul(h2_ps[m], w2_sb[:, k, P * m:P * m + P], h1_sb[:, k, :],
                                    start=(k == 0), stop=(k == M1 - 1))
                    if k == M1 - 1:
                        ins.then_inc(h2_summed, 1)
            for k in range(M2):
                pe.wait_ge(h2_ready, k + 1)
                ins = pe.matmul(out_ps, w3_sb[:, k:k + 1], h2_sb[:, k, :], start=(k == 0), stop=(k == M2 - 1))
            ins.then_inc(out_summed, 1)


def pair_numbers():
    return {p: n for n, p in enumerate(zip(*np.triu_indices(F, k=1)))}


def lay_out_pairs(w):
    number = pair_numbers()
    laid = np.zeros((CHUNKS, D, CHUNK, P), w.dtype)
    for t in range(NT):
        for i, j, rows, elements, _ in pairs_of(t):
            i, j = ORDER[i], ORDER[j]
            m = w[number[(i, j)]] if i < j else w[number[(j, i)]].T
            laid[t // CHUNK, :, t % CHUNK, rows] = m[:, elements]
    return laid.reshape(CHUNKS, D, CHUNK * P)


def lay_out_top1(w):
    number = pair_numbers()
    laid = np.zeros((P, BANKS, N1), w.dtype)
    for t in range(NT):
        for i, j, _, _, n in pairs_of(t):
            bank, row = z_row(t // 2, n)
            i, j = ORDER[i], ORDER[j]
            laid[row, bank] = w[number[(min(i, j), max(i, j))]]
    laid[DENSE_ROW:DENSE_ROW + N_DENSE, BANKS - 1] = w[len(number):]
    return laid


def kernel(**inputs):
    import concourse.bacc as _bacc
    from concourse.bass_utils import run_bass_kernel_spmd as _run

    a = {name: np.ascontiguousarray(x) for name, x in inputs.items()}
    arrays = {
        "in_ids": a["ids"],
        "in_ids_one_hot": np.ascontiguousarray(a["ids"][:, ONE_HOT_FIELDS].T),
        "in_row_numbers": np.arange(TABLE_ROWS, dtype=np.float32).reshape(TP, TK),
        **{f"in_tbl_{f}": a[f"tbl_{f}"] for f in range(F)},
        "in_dense_t": np.ascontiguousarray(a["dense_ctx"].T),
        "in_w_pairs": lay_out_pairs(a["L0_rec_W"]),
        "in_w1": lay_out_top1(a["W_top1"]),
        "in_b1": np.ascontiguousarray(a["b_top1"].reshape(M1, P).T),
        "in_w2": np.ascontiguousarray(a["W_top2"].reshape(M1, P, N2).transpose(1, 0, 2)),
        "in_b2": np.ascontiguousarray(a["b_top2"].reshape(M2, P).T),
        "in_w3": np.ascontiguousarray(a["W_top3"].reshape(M2, P).T),
    }
    nc = _bacc.Bacc("TRN2", target_bir_lowering=False, num_devices=1)
    ap = {name: nc.dram_tensor(name, x.shape, mybir.dt.from_np(x.dtype), kind="ExternalInput").ap()
          for name, x in arrays.items()}
    out = nc.dram_tensor("out_y", (B, 1), F32, kind="ExternalOutput").ap()
    dlrm_tower(nc, ap["in_ids"], ap["in_ids_one_hot"], ap["in_row_numbers"], [ap[f"in_tbl_{f}"] for f in range(F)], ap["in_dense_t"], ap["in_w_pairs"],
               ap["in_w1"], ap["in_b1"], ap["in_w2"], ap["in_b2"], ap["in_w3"], out)
    r = _run(nc, [arrays], core_ids=[0])
    return r.results[0]["out_y"]
```
